# Optimizing a Trainium2 kernel written in Bass

```python
import numpy as np
import jax
import jax.numpy as jnp

def _softmax(x, axis=-1):
    return jax.nn.softmax(x, axis=axis)

def _gelu(x):
    return jax.nn.gelu(x, approximate=True)

def _silu(x):
    return jax.nn.silu(x)

def _sigmoid(x):
    return jax.nn.sigmoid(x)

def _layernorm(x, axis=-1, eps=1e-05):
    m = jnp.mean(x, axis=axis, keepdims=True)
    v = jnp.var(x, axis=axis, keepdims=True)
    return (x - m) / jnp.sqrt(v + eps)

def _scatter_add(tgt, idx, src, axis=0):
    return tgt.at[idx].add(src)

def _segment_sum(src, seg, n):
    return jax.ops.segment_sum(src, seg, n)
kernel_name = 'mk_seq_postln_d1_jaxref_r4_d707af'

def setup_inputs(seed: int=0):
    np.random.seed(seed)
    _w = jnp.asarray

    def _L0_attn_setup():
        import jax, jax.numpy as jnp
        import numpy as np
        B, N, DIM_IN, DIM_INNER, DIM_OUT, WINDOW = (4, 1024, 256, 256, 256, 128)
        key = jax.random.key(seed)
        k1, k2, k3, k4 = jax.random.split(key, 4)
        x = jax.random.normal(k1, (B, N, DIM_IN), dtype=jnp.float32)
        w_qkv = jax.random.normal(k2, (DIM_IN, 3 * DIM_INNER), dtype=jnp.float32) / np.sqrt(DIM_IN)
        w_out = jax.random.normal(k3, (DIM_INNER, DIM_OUT), dtype=jnp.float32) / np.sqrt(DIM_INNER)
        b_out = jax.random.normal(k4, (DIM_OUT,), dtype=jnp.float32) * 0.01
        return {'x': x, 'w_qkv': w_qkv, 'w_out': w_out, 'b_out': b_out}
    _L0_attn_in = _L0_attn_setup()

    def _L0_ffn_setup():
        import jax, jax.numpy as jnp
        import numpy as np
        NUM_HEADS = 16
        TOP_K = 2
        ROPE_BASE = 10000.0
        LN_EPS = 1e-05

        def _rope_sin_cos(S, D, dtype):
            inv_freq = 1.0 / ROPE_BASE ** (jnp.arange(0, D, 2, dtype=jnp.float32) / D)
            freqs = jnp.arange(S, dtype=jnp.float32)[:, None] * inv_freq[None, :]
            sin = jnp.sin(freqs).astype(dtype)[None, :, None, :]
            cos = jnp.cos(freqs).astype(dtype)[None, :, None, :]
            return (sin, cos)

        def _apply_rope(x, sin, cos):
            x1, x2 = (x[..., 0::2], x[..., 1::2])
            r1 = x1 * cos - x2 * sin
            r2 = x1 * sin + x2 * cos
            return jnp.stack([r1, r2], axis=-1).reshape(x.shape)

        def _layer_norm(x, w, b):
            mu = jnp.mean(x, axis=-1, keepdims=True)
            var = jnp.mean(jnp.square(x - mu), axis=-1, keepdims=True)
            return (x - mu) * jax.lax.rsqrt(var + LN_EPS) * w + b
        key = jax.random.key(seed)
        ks = jax.random.split(key, 8)
        B, S, E, NE = (2, 512, 256, 8)
        s = 0.02
        return {'x': jax.random.normal(ks[0], (B, S, E), dtype=jnp.float32), 'in_proj_w': jax.random.normal(ks[1], (3 * E, E), dtype=jnp.float32) * s, 'in_proj_b': jnp.zeros((3 * E,), dtype=jnp.float32), 'out_proj_w': jax.random.normal(ks[2], (E, E), dtype=jnp.float32) * s, 'out_proj_b': jnp.zeros((E,), dtype=jnp.float32), 'gate_w': jax.random.normal(ks[3], (NE, E), dtype=jnp.float32) * s, 'gate_b': jnp.zeros((NE,), dtype=jnp.float32), 'expert_w': jax.random.normal(ks[4], (NE, E, E), dtype=jnp.float32) * s, 'expert_b': jnp.zeros((NE, E), dtype=jnp.float32), 'ln1_w': jnp.ones((E,), dtype=jnp.float32), 'ln1_b': jnp.zeros((E,), dtype=jnp.float32), 'ln2_w': jnp.ones((E,), dtype=jnp.float32), 'ln2_b': jnp.zeros((E,), dtype=jnp.float32)}
    _L0_ffn_in = _L0_ffn_setup()
    _d = {'L0_attn_x': _L0_attn_in['x'], 'L0_attn_w_qkv': _L0_attn_in['w_qkv'], 'L0_attn_w_out': _L0_attn_in['w_out'], 'L0_attn_b_out': _L0_attn_in['b_out'], 'L0_ffn_in_proj_w': _L0_ffn_in['in_proj_w'], 'L0_ffn_in_proj_b': _L0_ffn_in['in_proj_b'], 'L0_ffn_out_proj_w': _L0_ffn_in['out_proj_w'], 'L0_ffn_out_proj_b': _L0_ffn_in['out_proj_b'], 'L0_ffn_gate_w': _L0_ffn_in['gate_w'], 'L0_ffn_gate_b': _L0_ffn_in['gate_b'], 'L0_ffn_expert_w': _L0_ffn_in['expert_w'], 'L0_ffn_expert_b': _L0_ffn_in['expert_b'], 'L0_ffn_ln1_w': _L0_ffn_in['ln1_w'], 'L0_ffn_ln1_b': _L0_ffn_in['ln1_b'], 'L0_ffn_ln2_w': _L0_ffn_in['ln2_w'], 'L0_ffn_ln2_b': _L0_ffn_in['ln2_b']}
    _x0 = _d['L0_attn_x']
    _d['L0_attn_x'] = jax.random.normal(jax.random.fold_in(jax.random.key(seed), 1), (2, 2048, 256), dtype=_x0.dtype)
    del _x0
    return _d

def reference(L0_attn_x, L0_attn_w_qkv, L0_attn_w_out, L0_attn_b_out, L0_ffn_in_proj_w, L0_ffn_in_proj_b, L0_ffn_out_proj_w, L0_ffn_out_proj_b, L0_ffn_gate_w, L0_ffn_gate_b, L0_ffn_expert_w, L0_ffn_expert_b, L0_ffn_ln1_w, L0_ffn_ln1_b, L0_ffn_ln2_w, L0_ffn_ln2_b):

    def _L0_attn_ref(x, w_qkv, w_out, b_out):
        import jax, jax.numpy as jnp
        import numpy as np
        B, N, DIM_IN, DIM_INNER, DIM_OUT, WINDOW = (4, 1024, 256, 256, 256, 128)
        b, n, _ = x.shape
        w = WINDOW
        scale = DIM_INNER ** (-0.5)
        qkv = jnp.einsum('bnd,de->bne', x, w_qkv)
        q, k, v = jnp.split(qkv, 3, axis=-1)
        nw = n // w
        win = lambda t: t.reshape(b, nw, w, DIM_INNER)
        q, k, v = (win(q), win(k), win(v))
        kp = jnp.pad(k, ((0, 0), (1, 0), (0, 0), (0, 0)))
        k2 = jnp.concatenate([kp[:, :-1], kp[:, 1:]], axis=2)
        v2 = k2
        sim = jnp.einsum('bwid,bwjd->bwij', q, k2) * scale
        i, j = (w, 2 * w)
        mask = jnp.triu(jnp.ones((i, j), dtype=bool), j - i + 1)
        mask_value = -jnp.finfo(sim.dtype).max
        sim = jnp.where(mask[None, None], mask_value, sim)
        attn = jax.nn.softmax(sim, axis=-1)
        out = jnp.einsum('bwij,bwjd->bwid', attn, v2)
        out = out.reshape(b, n, DIM_INNER)[:, :n]
        return jnp.einsum('bnd,de->bne', out, w_out) + b_out

    def _L0_ffn_ref(x, in_proj_w, in_proj_b, out_proj_w, out_proj_b, gate_w, gate_b, expert_w, expert_b, ln1_w, ln1_b, ln2_w, ln2_b):
        import jax, jax.numpy as jnp
        import numpy as np
        NUM_HEADS = 16
        TOP_K = 2
        ROPE_BASE = 10000.0
        LN_EPS = 1e-05

        def _rope_sin_cos(S, D, dtype):
            inv_freq = 1.0 / ROPE_BASE ** (jnp.arange(0, D, 2, dtype=jnp.float32) / D)
            freqs = jnp.arange(S, dtype=jnp.float32)[:, None] * inv_freq[None, :]
            sin = jnp.sin(freqs).astype(dtype)[None, :, None, :]
            cos = jnp.cos(freqs).astype(dtype)[None, :, None, :]
            return (sin, cos)

        def _apply_rope(x, sin, cos):
            x1, x2 = (x[..., 0::2], x[..., 1::2])
            r1 = x1 * cos - x2 * sin
            r2 = x1 * sin + x2 * cos
            return jnp.stack([r1, r2], axis=-1).reshape(x.shape)

        def _layer_norm(x, w, b):
            mu = jnp.mean(x, axis=-1, keepdims=True)
            var = jnp.mean(jnp.square(x - mu), axis=-1, keepdims=True)
            return (x - mu) * jax.lax.rsqrt(var + LN_EPS) * w + b
        B, S, E = x.shape
        H = NUM_HEADS
        D = E // H
        xh = x.reshape(B, S, H, D)
        sin, cos = _rope_sin_cos(S, D, x.dtype)
        q_in = _apply_rope(xh, sin, cos).reshape(B, S, E)
        k_in = q_in
        v_in = x
        Wq, Wk, Wv = jnp.split(in_proj_w, 3, axis=0)
        bq, bk, bv = jnp.split(in_proj_b, 3, axis=0)
        q = (q_in @ Wq.T + bq).reshape(B, S, H, D)
        k = (k_in @ Wk.T + bk).reshape(B, S, H, D)
        v = (v_in @ Wv.T + bv).reshape(B, S, H, D)
        scale = 1.0 / jnp.sqrt(jnp.asarray(D, dtype=x.dtype))
        scores = jnp.einsum('bqhd,bkhd->bhqk', q, k) * scale
        causal = jnp.tril(jnp.ones((S, S), dtype=bool))
        scores = jnp.where(causal[None, None], scores, jnp.asarray(-jnp.inf, dtype=scores.dtype))
        attn = jax.nn.softmax(scores, axis=-1)
        ctx = jnp.einsum('bhqk,bkhd->bqhd', attn, v).reshape(B, S, E)
        attn_out = ctx @ out_proj_w.T + out_proj_b
        x1 = _layer_norm(x + attn_out, ln1_w, ln1_b)
        gates = jax.nn.softmax(x1 @ gate_w.T + gate_b, axis=-1)
        _, top_idx = jax.lax.top_k(gates, TOP_K)
        top_gates = jnp.take_along_axis(gates, top_idx, axis=-1)
        expert_outputs = jnp.einsum('bsd,efd->bsef', x1, expert_w) + expert_b[None, None]
        sel = jnp.take_along_axis(expert_outputs, top_idx[..., None], axis=2)
        moe_out = jnp.sum(sel * top_gates[..., None], axis=2)
        return _layer_norm(x1 + moe_out, ln2_w, ln2_b)
    x = L0_attn_x
    x = _layernorm(x + _L0_attn_ref(x, L0_attn_w_qkv, L0_attn_w_out, L0_attn_b_out), axis=-1)
    x = _layernorm(x + _L0_ffn_ref(x, L0_ffn_in_proj_w, L0_ffn_in_proj_b, L0_ffn_out_proj_w, L0_ffn_out_proj_b, L0_ffn_gate_w, L0_ffn_gate_b, L0_ffn_expert_w, L0_ffn_expert_b, L0_ffn_ln1_w, L0_ffn_ln1_b, L0_ffn_ln2_w, L0_ffn_ln2_b), axis=-1)
    return x

_drawn_inputs = setup_inputs


def setup_inputs(seed=0):
    import zlib

    import numpy as np

    out = dict(_drawn_inputs(seed))
    spreads = {'L0_ffn_in_proj_b': (0.0, 0.44),
     'L0_ffn_out_proj_b': (0.0, 0.1),
     'L0_ffn_gate_b': (0.0, 0.323),
     'L0_ffn_expert_b': (0.0, 0.646),
     'L0_ffn_ln1_w': (1.0, 0.2),
     'L0_ffn_ln1_b': (0.0, 0.1),
     'L0_ffn_ln2_w': (1.0, 0.2),
     'L0_ffn_ln2_b': (0.0, 0.1)}
    factors = {'L0_attn_b_out': 5.217, 'L0_ffn_in_proj_w': 8.0, 'L0_ffn_out_proj_w': 3.082}
    for name, (base, spread) in spreads.items():
        noise = np.random.default_rng([zlib.crc32(name.encode()), seed]).standard_normal(out[name].shape)
        drawn = base * np.exp(spread * noise) if base else spread * noise
        out[name] = jnp.asarray(drawn.astype(out[name].dtype))
    for name, factor in factors.items():
        out[name] = (out[name] * factor).astype(out[name].dtype)
    return out
```

```python
from contextlib import ExitStack

import numpy as np
import concourse.bass as bass
from concourse import mybir

F32 = mybir.dt.float32
BF16 = mybir.dt.bfloat16
U32 = mybir.dt.uint32
ALU = mybir.AluOpType
ACT = mybir.ActivationFunctionType
AX_X = mybir.AxisListType.X

P = 128
E = 256
EC = E // P
B, N = 2, 2048
H, DH = 16, 16
DV = DH + 1
TB = N // P
NT = B * TB
GT = 4
GQ = GT * P
GB = TB // GT
NG = B * GB
HJ = 4
NE = 8
SLOTS = 6
KR = SLOTS * DH
NPART = 3
Q_PARTS = (0, 0, 0, 1, 1, 2)
K_PARTS = (0, 1, 2, 0, 1, 0)
KRING = GB + 1
QRING = 2
MXB, STB = 2, 3
PB = 8
NEG = -1.0e30
EPS = 1e-5
NCHAINM = 5
NTOP = 7


def ds(start, size):
    return slice(start, start + size) if isinstance(start, int) else bass.ds(start, size)


def is_first(count):
    return isinstance(count, int) and count == 0


def keys_groups(s):
    return s % GB + 1


def units(s):
    return 16 * keys_groups(s)


def units_before(s, hg):
    return sum(HJ * units(x) for x in range(s)) + hg * units(s)


def key_tiles(s):
    return GT * keys_groups(s)


def key_tiles_before(s, hg):
    return sum(HJ * key_tiles(x) for x in range(s)) + hg * key_tiles(s)


def loads_before(s, hg, c):
    return sum(4 for x in range(s) if x % GB >= c) + hg


A_CHAIN = """a_xT a_xTc a_xb a_q a_qc a_s a_max a_exp a_pT a_pTc a_y a_yc a_load a_o a_res a_rstd a_norm
a_st0 a_rope a_load_cs a_rT a_rTc a_qk a_qkf a_v a_vst a_vstore a_split a_pst . a_stack""".split()
D_CHAIN = """d_load . d_cp d_cT d_cTc d_xb d_o d_res d_rstd d_norm d_aff d_x1T d_x1Tc d_g d_lg d_gexp d_top d_wT d_wTc
d_b d_acc0 d_e0 d_e0c d_e1 d_e1c d_e1a d_e2 d_e2c d_e3 d_e3c d_e3a d_y d_rstd2 d_norm2 d_aff2 d_z d_rstd3
d_norm3 d_store""".split()


def spread(lists):
    at = []
    for k, (steps, start, end) in enumerate(lists):
        for i, x in enumerate(steps):
            at.append((start + (end - start) * (i + 0.5) / len(steps), k, i, x))
    return [x for _, _, _, x in sorted(at) if x[0] != "."]


def order(mx_s, st_s, has_a, has_d, hold_stack):
    lists = []
    if mx_s is not None:
        g = keys_groups(mx_s)
        lists.append(([("mx", c, j, h) for c in range(g) for j in range(GT) for h in range(HJ)], -0.08, 0.82))
        lists.append(([("nm_d",), ("nm_T",)], 0.80, 1.0))
    if st_s is not None:
        g, st = keys_groups(st_s), []
        for kb in range(GT * g):
            st += [("st", kb, h) for h in range(HJ)]
            if kb:
                st.append(("pv", kb - 1))
                if kb % GT == 0:
                    st.append(("vload", kb // GT - 1))
        st += [("pv", GT * g - 1), ("vload", g - 1)]
        lists.append((st, 0.04, 1.0))
    a = [(x,) for x in A_CHAIN if not (hold_stack and x == "a_stack")]
    if has_a:
        lists.append((a, -0.08, 0.90))
    if has_d:
        lists.append(([(x,) for x in D_CHAIN], -0.08, 0.95))
    steps = [("vload_new",)] + spread(lists)
    if mx_s is not None and has_a:
        assert steps.index(("a_vst",)) < steps.index(("nm_T",))
    if has_a and hold_stack:
        steps.append(("a_stack",))
    if st_s is not None:
        steps += [("o_evac",), ("o_T",), ("o_ctx",)]
    return steps


class Turn:

    def __init__(self, s, u):
        first = is_first(u)
        self.s, self.u = s, u
        self.mx = (s, u) if 0 <= s < NG else None
        if first:
            self.st = (s - 1, 3) if s >= 1 else None
            self.dt = (s - 2, 3) if s >= 2 else None
        else:
            self.st = (s, u - 1) if 0 <= s < NG else None
            self.dt = (s - 1, u - 1) if s >= 1 else None
        self.at = (s + 1, u) if s < NG - 1 else None
        self.steps = order(self.mx and s, self.st and self.st[0], self.at is not None, self.dt is not None,
                           first and s >= 1)


def walk(eng, body):
    for s in range(-1, NG + 1):
        written = 2 if s in (0, 1) else 1
        for u in range(written):
            body(Turn(s, u))
        with eng.Fori(written, 5 if s == NG else 4) as u:
            body(Turn(s, u))


def build(nc, windows, cs, w_qk_t, w_out, in_t, in_b, wo_t, gate_t, exp_t, exp_b, rows, gate_b, out):
    x0_dram = nc.dram_tensor("x0_scratch", (NT * P, E), F32, kind="Internal").ap()
    v_dram = nc.dram_tensor("v_scratch", (NT * P, H * DV), F32, kind="Internal").ap()
    parts_dram = nc.dram_tensor("parts_scratch", (NT * NPART * 2 * E, P), BF16, kind="Internal").ap()

    with ExitStack() as ctx:
        def sb(name, shape, dt=F32):
            return ctx.enter_context(nc.sbuf_tensor(name, shape, dt))

        def sem(name):
            return ctx.enter_context(nc.semaphore(name))

        idf = sb("idf", [P, P])
        idb = sb("idb", [P, P], BF16)
        maskb = sb("maskb", [P, P], BF16)
        iota8 = sb("iota8", [P, NE])
        mhalf = sb("mhalf", [P, 1])
        m_sb = sb("m_sb", [P, EC, E])
        wko = sb("wko", [P, EC, E])
        inw = sb("inw", [P, EC, 3 * E])
        wo = sb("wo", [P, EC, E])
        gw = sb("gw", [P, EC, NE])
        ew = sb("ew", [P, EC, NE * E])
        eb = sb("eb", [NE, E])
        qkb = sb("qkb", [P, 2 * EC])
        rowv = sb("rowv", [P, 7, E])
        gb_sb = sb("gb_sb", [P, NE])
        b_out, b_v, b_op, g1, b1, g2, b2 = (rowv[:, i, :] for i in range(7))

        qs = sb("qs", [P, H * QRING * GQ], BF16)
        ks = sb("ks", [P, H * KRING * GQ], BF16)
        qs3 = qs[:, :].rearrange("p (h c) -> p h c", h=H)
        ks3 = ks[:, :].rearrange("p (h c) -> p h c", h=H)
        vcur = sb("vcur", [P, TB, HJ, DV])
        pbuf = sb("pbuf", [P, PB, GQ])
        mxs = sb("mxs", [P, GT * HJ, GB])
        nm = sb("nm", [P, GT * HJ])
        nmd = sb("nmd", [P, GT * HJ])
        nmp = sb("nmp", [P, GT, HJ, NPART], BF16)
        nmT = sb("nmT", [NPART * HJ, GQ], BF16)
        osb = sb("osb", [P, GQ])
        oden = sb("oden", [P, GT, HJ])
        ctxn = sb("ctxn", [P, 2 * GT, E])

        xw = sb("xw", [P, 2, E])
        cst = sb("cst", [P, 2, DH])
        xb = sb("xb", [P, E])
        xT = sb("xT", [P, EC, 2 * P])
        qT = sb("qT", [P, EC, P])
        nmA = sb("nmA", [P, 1])
        sumA = sb("sumA", [P, 1])
        rsA = sb("rsA", [P, 1])
        pA = sb("pA", [P, 2 * P])
        pT = pA[:, :].rearrange("p (w t) -> p w t", w=2)
        yT = qT
        rA = xb
        stA = sb("stA", [P, 6])
        mvA = sb("mvA", [P, 2])
        veA = sb("veA", [P, 1])
        rstdA = sb("rstdA", [P, 1])
        x0 = sb("x0", [P, E])
        rp = pA
        rxT = xT[:, :, :].rearrange("p c (w t) -> p (c w) t", w=2)
        qkf = sb("qkf", [P, 2 * EC, P])
        qkr = sb("qkr", [P, 2 * EC, P])
        rps = qkr[:, 0:2, :].rearrange("p c t -> p (c t)")
        parts = sb("parts", [P, NPART, 2 * EC, P], BF16)
        vst = sb("vst", [P, H, DV])

        x0d = sb("x0d", [P, E])
        x0b = sb("x0b", [P, E])
        cj = sb("cj", [P, E])
        cT = sb("cT", [P, EC, P])
        rD = sb("rD", [P, E])
        stD = sb("stD", [P, 6])
        mvD = sb("mvD", [P, 2])
        veD = sb("veD", [P, 1])
        rstdD = sb("rstdD", [P, 1])
        xh = x0b
        x1 = sb("x1", [P, E])
        x1T = cT
        lg = sb("lg", [P, NE])
        ngm = sb("ngm", [P, 1])
        ge = sb("ge", [P, NE])
        gsum = sb("gsum", [P, 1])
        gr = sb("gr", [P, 1])
        gates = sb("gates", [P, NE])
        top8 = sb("top8", [P, 8])
        ix8 = sb("ix8", [P, 8], U32)
        ixf = sb("ixf", [P, 8])
        w1st = sb("w1st", [P, NE])
        w2nd = sb("w2nd", [P, NE])
        wts = sb("wts", [P, NE])
        wT = sb("wT", [NE, P])
        acc = sb("acc", [P, E])
        etmp = sb("etmp", [P, 2, E])
        accp = cj
        obuf = x1

        bank = [ctx.enter_context(nc.psum_tensor(f"bank{i}", [P, 512], F32)) for i in range(8)]
        mxbank, stbank, obank, abank, dbank = bank[0:MXB], bank[MXB:MXB + STB], bank[5], bank[6], bank[7]
        nmbank = abank[0:NPART * HJ, 0:GQ // 2].bitcast(BF16)

        fold_loaded = sem("fold_loaded")
        proj_loaded = sem("proj_loaded")
        moe_loaded = sem("moe_loaded")
        ones_loaded = sem("ones_loaded")
        consts = sem("consts")
        fold_ps = sem("fold_ps")
        folded = sem("folded")
        dve_set = sem("dve_set")
        mx_ready = sem("mx_ready")
        mx_used = sem("mx_used")
        nm_step = sem("nm_step")
        nmT_ps = sem("nmT_ps")
        nmT_ready = sem("nmT_ready")
        nm_loaded = sem("nm_loaded")
        st_ready = sem("st_ready")
        exp_done = sem("exp_done")
        pv_done = sem("pv_done")
        vcur_loaded = [sem(f"vcur_loaded{c}") for c in range(GB)]
        osb_ready = sem("osb_ready")
        oT_ps = sem("oT_ps")
        oden_ready = sem("oden_ready")
        ctx_ready = sem("ctx_ready")
        xw_loaded = sem("xw_loaded")
        cs_loaded = sem("cs_loaded")
        xT_ps = sem("xT_ps")
        xT_ready = sem("xT_ready")
        xb_ready = sem("xb_ready")
        qT_ps = sem("qT_ps")
        qT_ready = sem("qT_ready")
        sA_ps = sem("sA_ps")
        nmA_ready = sem("nmA_ready")
        pA_ready = sem("pA_ready")
        pT_ps = sem("pT_ps")
        pT_ready = sem("pT_ready")
        yT_ps = sem("yT_ps")
        yT_ready = sem("yT_ready")
        oA_ps = sem("oA_ps")
        rsA_ready = sem("rsA_ready")
        rA_ready = sem("rA_ready")
        stA_ready = sem("stA_ready")
        mvA_ready = sem("mvA_ready")
        veA_ready = sem("veA_ready")
        rstdA_ready = sem("rstdA_ready")
        x0_ready = sem("x0_ready")
        x0_stored = sem("x0_stored")
        rope_step = sem("rope_step")
        rp_ready = sem("rp_ready")
        rxT_ps = sem("rxT_ps")
        rxT_ready = sem("rxT_ready")
        qk_ps = sem("qk_ps")
        qkf_ready = sem("qkf_ready")
        v_ps = sem("v_ps")
        vst_ready = sem("vst_ready")
        v_stored = sem("v_stored")
        split_step = sem("split_step")
        parts_ready = sem("parts_ready")
        parts_stored = sem("parts_stored")
        stack_loaded = sem("stack_loaded")
        x0d_loaded = sem("x0d_loaded")
        cj_ready = sem("cj_ready")
        cT_ps = sem("cT_ps")
        cT_ready = sem("cT_ready")
        x0b_ready = sem("x0b_ready")
        oD_ps = sem("oD_ps")
        rD_ready = sem("rD_ready")
        stD_ready = sem("stD_ready")
        mvD_ready = sem("mvD_ready")
        veD_ready = sem("veD_ready")
        rstdD_ready = sem("rstdD_ready")
        xh_ready = sem("xh_ready")
        aff_step = sem("aff_step")
        x1_ready = sem("x1_ready")
        x1T_ps = sem("x1T_ps")
        x1T_ready = sem("x1T_ready")
        g_ps = sem("g_ps")
        lg_ready = sem("lg_ready")
        ngm_ready = sem("ngm_ready")
        ge_ready = sem("ge_ready")
        top_step = sem("top_step")
        wts_ready = sem("wts_ready")
        wT_ps = sem("wT_ps")
        wT_ready = sem("wT_ready")
        eb_ps = sem("eb_ps")
        acc_step = sem("acc_step")
        e_ps = sem("e_ps")
        etmp_ready = sem("etmp_ready")
        accp_step = sem("accp_step")
        z_ready = sem("z_ready")
        ob_ready = sem("ob_ready")
        out_stored = sem("out_stored")

        waited = {e.engine: sem(f"waited_{i}") for i, e in enumerate((nc.sync, nc.gpsimd, nc.vector))}
        FOLD_LOADS, PROJ_LOADS, MOE_LOADS = 2, 3, 6

        def settled(eng):
            eng.sem_inc(waited[eng.engine], 1)

        block = ctx.enter_context(nc.Block())

        @block.sync
        def _(sp):
            wqkt = pbuf[:, 0:2, :].rearrange("p a b -> p (a b)").rearrange("p (c d) -> p c d", c=2 * EC)
            woutn = pbuf[:, 2, :].rearrange("p (c d) -> p c d", c=EC)

            def load_windows(T):
                sp.dma_start(xw[:, :, :], windows[ds(T * (2 * P), 2 * P), :].rearrange("(w p) d -> p w d", p=P))\
                    .then_inc(xw_loaded, 16)

            def load_angles(T):
                sp.dma_start(cst[:, :, :].rearrange("p k i -> p (k i)"), cs[ds(T * P, P), :]).then_inc(cs_loaded, 16)

            for dst, src in ((wqkt, w_qk_t.rearrange("(c p) d -> p c d", p=P)),
                             (woutn, w_out.rearrange("(c p) d -> p c d", p=P))):
                sp.dma_start(dst, src).then_inc(fold_loaded, 16)
            load_windows(0)
            for dst, src in ((inw[:, :, :], in_t.rearrange("(c p) d -> p c d", p=P)), (qkb[:, :], in_b),
                             (rowv[:, :, :], rows)):
                sp.dma_start(dst, src).then_inc(proj_loaded, 16)
            load_angles(0)
            sp.wait_ge(dve_set, 2)
            sp.dma_start(ks3[KR:KR + NPART, 1:H, :],
                         ks3[KR:KR + NPART, 0:1, :].broadcast_to([NPART, H - 1, KRING * GQ])).then_inc(ones_loaded, 16)
            for dst, src in (
                (wo[:, :, :], wo_t.rearrange("(c p) d -> p c d", p=P)),
                (gw[:, :, :], gate_t.rearrange("(c p) d -> p c d", p=P)),
                (gb_sb[:, :], gate_b),
                (eb[:, :], exp_b),
                (ew[:, 0, :], exp_t[0:P, :]),
                (ew[:, 1, :], exp_t[P:2 * P, :]),
            ):
                sp.dma_start(dst, src).then_inc(moe_loaded, 16)

            def body(t):
                if t.at:
                    sa, ua = t.at
                    T = GT * sa + ua
                if t.dt:
                    sd, ud = t.dt
                    TD = GT * sd + ud
                for step in t.steps:
                    name = step[0]
                    if name == "a_load":
                        sp.wait_ge(xb_ready, T + 1)
                        sp.wait_ge(yT_ps, T + 1)
                        load_windows(T + 1)
                    elif name == "a_load_cs":
                        sp.wait_ge(rp_ready, T + 1)
                        load_angles(T + 1)
                    elif name == "a_st0":
                        sp.wait_ge(x0_ready, T + 1)
                        sp.dma_start(x0_dram[ds(T * P, P), :], x0[:, :]).then_inc(x0_stored, 16)
                    elif name == "a_vstore":
                        sp.wait_ge(vst_ready, T + 1)
                        sp.dma_start(v_dram[ds(T * P, P), :], vst[:, :, :].rearrange("p h d -> p (h d)"))\
                            .then_inc(v_stored, 16)
                    elif name == "a_pst":
                        sp.wait_ge(parts_ready, T + 1)
                        sp.dma_start(parts_dram[ds(T * (NPART * 2 * E), NPART * 2 * E), :]
                                     .rearrange("(x p) t -> p x t", p=P),
                                     parts[:, :, :, :].rearrange("p a c t -> p (a c) t")).then_inc(parts_stored, 16)
                    elif name == "a_stack":
                        sp.wait_ge(parts_stored, 16 * (T + 1))
                        if is_first(ua) and sa >= 2:
                            sp.wait_ge(pv_done, key_tiles_before(sa - 1, 0))
                        for q, (dst, ring, a_of) in enumerate(((qs3, QRING, Q_PARTS), (ks3, KRING, K_PARTS))):
                            col = (sa % ring) * GQ + ua * P
                            for slot, a in enumerate(a_of):
                                r0 = T * (NPART * 2 * E) + (a * 2 + q) * E
                                sp.dma_start(dst[slot * DH:(slot + 1) * DH, :, ds(col, P)],
                                             parts_dram[ds(r0, E), :].rearrange("(h d) t -> d h t", d=DH))\
                                    .then_inc(stack_loaded, 16)
                    elif name in ("vload_new", "vload"):
                        if not t.mx:
                            continue
                        sm, um = t.mx
                        held = keys_groups(t.st[0]) if t.st else 0
                        if name == "vload_new":
                            if is_first(um):
                                sp.wait_ge(v_stored, 16 * GT * (sm + 1))
                            if t.st and held < keys_groups(sm):
                                sp.wait_ge(pv_done, key_tiles_before(*t.st))
                            chunks = range(held, keys_groups(sm))
                        else:
                            c = step[1]
                            chunks = [c] if c < keys_groups(sm) else []
                            if chunks:
                                sp.wait_ge(pv_done, key_tiles_before(*t.st) + GT * (c + 1))
                        for c in chunks:
                            r0 = ((sm // GB) * TB + c * GT) * P
                            sp.dma_start(vcur[:, GT * c:GT * (c + 1), :, :].rearrange("p k h d -> p k (h d)"),
                                         v_dram[r0:r0 + GT * P, ds(um * (HJ * DV), HJ * DV)]
                                         .rearrange("(k p) x -> p k x", p=P)).then_inc(vcur_loaded[c], 16)
                    elif name == "nm_T":
                        sm, um = t.mx
                        sp.wait_ge(nmT_ready, GT * sm + um + 1)
                        for h in range(HJ):
                            sp.dma_start(qs[KR:KR + NPART, ds((um * HJ + h) * (QRING * GQ) + (sm % QRING) * GQ, GQ)],
                                         nmT[h * NPART:(h + 1) * NPART, :]).then_inc(nm_loaded, 16)
                    elif name == "d_load":
                        sp.wait_ge(x0_stored, 16 * (TD + 1))
                        settled(sp)
                        if not is_first(TD):
                            sp.wait_ge(z_ready, TD)
                        sp.dma_start(x0d[:, :], x0_dram[ds(TD * P, P), :]).then_inc(x0d_loaded, 16)
                    elif name == "d_store":
                        sp.wait_ge(ob_ready, TD + 1)
                        sp.dma_start(out[ds(TD * P, P), :], obuf[:, :]).then_inc(out_stored, 16)

            walk(sp, body)
            sp.wait_ge(xw_loaded, 16 * (NT + 1))
            sp.wait_ge(cs_loaded, 16 * (NT + 1))
            sp.wait_ge(x0_stored, 16 * NT)
            sp.wait_ge(v_stored, 16 * NT)
            sp.wait_ge(parts_stored, 16 * NT)
            sp.wait_ge(out_stored, 16 * NT)

        @block.gpsimd
        def _(pool):
            pool.memset(idf[:, :], 0.0).then_inc(consts, 1)
            pool.memset(idb[:, :], 0.0).then_inc(consts, 1)
            pool.memset(maskb[:, :], 0.0).then_inc(consts, 1)
            pool.memset(mhalf[:, :], -0.5).then_inc(consts, 1)
            pool.memset(vst[:, :, :], 1.0).then_inc(consts, 1)
            pool.iota(iota8[:, :], pattern=[[1, NE]], base=0, channel_multiplier=0,
                      allow_small_or_imprecise_dtypes=True).then_inc(consts, 1)
            pool.wait_ge(consts, 6)
            for m in (idf, idb):
                pool.affine_select(out=m[:, :], in_=m[:, :], compare_op=ALU.not_equal, fill=1.0, base=0,
                                   pattern=[[-1, P]], channel_multiplier=1).then_inc(consts, 1)
            pool.affine_select(out=maskb[:, :], in_=maskb[:, :], compare_op=ALU.is_ge, fill=NEG, base=0,
                               pattern=[[-1, P]], channel_multiplier=1).then_inc(consts, 1)
            pool.wait_ge(proj_loaded, 16 * PROJ_LOADS)

            def body(t):
                if t.at:
                    T = GT * t.at[0] + t.at[1]
                if t.dt:
                    sd, ud = t.dt
                    TD = GT * sd + ud
                for step in t.steps:
                    name = step[0]
                    if name == "a_xb":
                        pool.wait_ge(xw_loaded, 16 * (T + 1))
                        if not is_first(T):
                            pool.wait_ge(x0_ready, T)
                        pool.tensor_tensor(xb[:, :], xw[:, 1, :], b_out, ALU.add).then_inc(xb_ready, 1)
                    elif name == "a_rstd":
                        pool.wait_ge(mvA_ready, T + 1)
                        settled(pool)
                        pool.tensor_scalar(veA[:, :], mvA[:, 1:2], EPS, None, ALU.add).then_inc(veA_ready, 1)
                        pool.wait_ge(veA_ready, T + 1)
                        pool.tensor_tensor(rstdA[:, :], veA[:, :], mhalf[:, :], ALU.pow).then_inc(rstdA_ready, 1)
                    elif name == "a_rope":
                        pool.wait_ge(x0_ready, T + 1)
                        pool.wait_ge(cs_loaded, 16 * (T + 1))
                        if not is_first(T):
                            pool.wait_ge(rxT_ps, T)
                        xv = x0[:, :].rearrange("p (h i e) -> p h i e", h=H, e=2)
                        cosv = cst[:, 0, :].unsqueeze(1).broadcast_to([P, H, DH])
                        sv = cst[:, 1, :].rearrange("p (i e) -> p i e", e=2)
                        rsv = rps.rearrange("p (h i e) -> p h i e", h=H, e=2)
                        pool.tensor_tensor(rp[:, :].rearrange("p (h i) -> p h i", h=H),
                                           x0[:, :].rearrange("p (h i) -> p h i", h=H), cosv, ALU.mult)\
                            .then_inc(rope_step, 1)
                        for e in range(2):
                            pool.tensor_tensor(rsv[:, :, :, e], xv[:, :, :, 1 - e],
                                               sv[:, :, e].unsqueeze(1).broadcast_to([P, H, DH // 2]), ALU.mult)\
                                .then_inc(rope_step, 1)
                        pool.wait_ge(rope_step, 3 * (T + 1))
                        pool.tensor_tensor(rp[:, :], rp[:, :], rps, ALU.add).then_inc(rp_ready, 1)
                    elif name == "a_split":
                        pool.wait_ge(qkf_ready, T + 1)
                        if not is_first(T):
                            pool.wait_ge(parts_stored, 16 * T)
                        settled(pool)
                        pool.tensor_copy(parts[:, 0, :, :], qkf[:, :, :]).then_inc(split_step, 1)
                        pool.wait_ge(split_step, 3 * T + 1)
                        pool.tensor_tensor(qkr[:, :, :], qkf[:, :, :], parts[:, 0, :, :], ALU.subtract)\
                            .then_inc(split_step, 1)
                        pool.wait_ge(split_step, 3 * T + 2)
                        settled(pool)
                        pool.tensor_copy(parts[:, 1, :, :], qkr[:, :, :]).then_inc(split_step, 1)
                        pool.wait_ge(split_step, 3 * T + 3)
                        pool.tensor_tensor(parts[:, 2, :, :], qkr[:, :, :], parts[:, 1, :, :], ALU.subtract)\
                            .then_inc(parts_ready, 1)
                    elif name == "d_cp":
                        pool.wait_ge(ctx_ready, GT * (sd + 1))
                        if not is_first(TD):
                            pool.wait_ge(rD_ready, 2 * TD)
                        settled(pool)
                        pool.tensor_copy(cj[:, :], ctxn[:, ds((sd % 2) * GT + ud, 1), :]
                                         .rearrange("p a b -> p (a b)")).then_inc(cj_ready, 1)
                    elif name == "d_xb":
                        pool.wait_ge(x0d_loaded, 16 * (TD + 1))
                        pool.tensor_tensor(x0b[:, :], x0d[:, :], b_op, ALU.add).then_inc(x0b_ready, 1)
                    elif name in ("d_rstd", "d_rstd2", "d_rstd3"):
                        k = ("d_rstd", "d_rstd2", "d_rstd3").index(name) + 1
                        pool.wait_ge(mvD_ready, 3 * TD + k)
                        settled(pool)
                        pool.tensor_scalar(veD[:, :], mvD[:, 1:2], EPS, None, ALU.add).then_inc(veD_ready, 1)
                        pool.wait_ge(veD_ready, 3 * TD + k)
                        pool.tensor_tensor(rstdD[:, :], veD[:, :], mhalf[:, :], ALU.pow).then_inc(rstdD_ready, 1)
                    elif name == "d_aff":
                        pool.wait_ge(xh_ready, 2 * TD + 1)
                        pool.tensor_tensor(xh[:, :], xh[:, :], g1, ALU.mult).then_inc(aff_step, 1)
                        pool.wait_ge(aff_step, 3 * TD + 1)
                        if not is_first(TD):
                            pool.wait_ge(out_stored, 16 * TD)
                        pool.tensor_tensor(x1[:, :], xh[:, :], b1, ALU.add).then_inc(x1_ready, 1)
                    elif name == "d_e1a":
                        pool.wait_ge(etmp_ready, 2 * TD + 1)
                        pool.tensor_tensor(accp[:, :], etmp[:, 0, :], etmp[:, 1, :], ALU.add).then_inc(accp_step, 1)
                    elif name == "d_e3a":
                        pool.wait_ge(etmp_ready, 2 * TD + 2)
                        pool.wait_ge(accp_step, 3 * TD + 1)
                        pool.tensor_tensor(accp[:, :], accp[:, :], etmp[:, 0, :], ALU.add).then_inc(accp_step, 1)
                        pool.wait_ge(accp_step, 3 * TD + 2)
                        pool.tensor_tensor(accp[:, :], accp[:, :], etmp[:, 1, :], ALU.add).then_inc(accp_step, 1)
                    elif name == "d_aff2":
                        pool.wait_ge(xh_ready, 2 * TD + 2)
                        pool.tensor_tensor(xh[:, :], xh[:, :], g2, ALU.mult).then_inc(aff_step, 1)
                        pool.wait_ge(aff_step, 3 * TD + 2)
                        pool.tensor_tensor(xh[:, :], xh[:, :], b2, ALU.add).then_inc(aff_step, 1)
                        pool.wait_ge(aff_step, 3 * TD + 3)
                        pool.tensor_tensor(rD[:, :], xh[:, :], x0d[:, :], ALU.add).then_inc(z_ready, 1)

            walk(pool, body)

        @block.scalar
        def _(act):
            def copy(o, i, scale=1.0):
                return nc.scalar.activation(o, i, ACT.Copy, scale=scale)

            for k, w in enumerate((m_sb, wko)):
                act.wait_ge(fold_ps, k + 1)
                copy(w[:, :, :], bank[k][:, :].rearrange("p (c d) -> p c d", c=EC)).then_inc(folded, 1)

            def body(t):
                if t.at:
                    T = GT * t.at[0] + t.at[1]
                if t.dt:
                    TD = GT * t.dt[0] + t.dt[1]
                for step in t.steps:
                    name = step[0]
                    if name == "st":
                        sj, hg = t.st
                        kb, h = step[1:]
                        i = kb * HJ + h
                        base = units_before(sj, hg)
                        r0 = max(0, kb - (key_tiles(sj) - GT)) * P
                        act.wait_ge(st_ready, base + i + 1)
                        if h == 0 and not (is_first(base) and kb < 2):
                            act.wait_ge(pv_done, key_tiles_before(sj, hg) + kb - 1)
                        nc.scalar.activation(pbuf[:, i % PB, r0:GQ], stbank[i % STB][:, r0:GQ], ACT.Exp)\
                            .then_inc(exp_done, 1)
                    elif name == "nm_T":
                        job = GT * t.mx[0] + t.mx[1]
                        act.wait_ge(nmT_ps, job + 1)
                        if not is_first(job):
                            act.wait_ge(nm_loaded, 16 * HJ * job)
                        copy(nmT[:, :], nmbank).then_inc(nmT_ready, 1)
                    elif name == "o_evac":
                        act.wait_ge(pv_done, key_tiles_before(*t.st) + key_tiles(t.st[0]))
                        copy(osb[:, :], obank[:, :]).then_inc(osb_ready, 1)
                    elif name == "a_xTc":
                        act.wait_ge(xT_ps, T + 1)
                        copy(xT[:, :, :], abank[:, :].rearrange("p (c t) -> p c t", c=EC)).then_inc(xT_ready, 1)
                    elif name == "a_qc":
                        act.wait_ge(qT_ps, T + 1)
                        copy(qT[:, :, :], abank[:, 0:E].rearrange("p (c t) -> p c t", c=EC), E ** -0.5)\
                            .then_inc(qT_ready, 1)
                    elif name == "a_exp":
                        act.wait_ge(nmA_ready, T + 1)
                        nc.scalar.activation(pA[:, :], abank[:, 0:2 * P], ACT.Exp, bias=nmA[:, 0:1],
                                             accum_out=sumA[:, 0:1]).then_inc(pA_ready, 1)
                    elif name == "a_pTc":
                        act.wait_ge(pT_ps, T + 1)
                        copy(pT, abank[:, 0:2 * P].rearrange("p (c t) -> p c t", c=2)).then_inc(pT_ready, 1)
                    elif name == "a_yc":
                        act.wait_ge(yT_ps, T + 1)
                        copy(yT[:, :, :], abank[:, 0:E].rearrange("p (c t) -> p c t", c=EC)).then_inc(yT_ready, 1)
                    elif name == "a_rTc":
                        act.wait_ge(rxT_ps, T + 1)
                        copy(rxT, abank[:, :].rearrange("p (c t) -> p c t", c=2 * EC)).then_inc(rxT_ready, 1)
                    elif name == "d_cTc":
                        act.wait_ge(cT_ps, TD + 1)
                        copy(cT[:, :, :], dbank[:, 0:E].rearrange("p (c t) -> p c t", c=EC)).then_inc(cT_ready, 1)
                    elif name == "d_x1Tc":
                        act.wait_ge(x1T_ps, TD + 1)
                        copy(x1T[:, :, :], dbank[:, 0:E].rearrange("p (c t) -> p c t", c=EC)).then_inc(x1T_ready, 1)
                    elif name == "d_gexp":
                        act.wait_ge(ngm_ready, TD + 1)
                        nc.scalar.activation(ge[:, :], lg[:, :], ACT.Exp, bias=ngm[:, 0:1], accum_out=gsum[:, 0:1])\
                            .then_inc(ge_ready, 1)
                    elif name == "d_wTc":
                        act.wait_ge(wT_ps, TD + 1)
                        copy(wT[:, :], dbank[0:NE, 0:P]).then_inc(wT_ready, 1)
                    elif name in ("d_e1c", "d_e3c"):
                        k = int(name[3])
                        act.wait_ge(e_ps, 4 * TD + k + 1)
                        if name == "d_e3c":
                            act.wait_ge(accp_step, 3 * TD + 1)
                        elif not is_first(TD):
                            act.wait_ge(accp_step, 3 * TD)
                        copy(etmp[:, 0, :], dbank[:, 0:E], wts[:, 2 * k:2 * k + 1])
                        copy(etmp[:, 1, :], dbank[:, E:2 * E], wts[:, 2 * k + 1:2 * k + 2]).then_inc(etmp_ready, 1)

            walk(act, body)

        @block.vector
        def _(dve):
            v = nc.vector
            v.memset(obank[:, :], 0.0).then_inc(dve_set, 1)
            v.memset(ks3[KR:KR + NPART, 0, :], 1.0).then_inc(dve_set, 1)
            dve.wait_ge(proj_loaded, 16 * PROJ_LOADS)
            v.tensor_scalar(inw[:, :, 0:E], inw[:, :, 0:E], DH ** -0.5, None, ALU.mult).then_inc(dve_set, 1)
            v.tensor_scalar(qkb[:, 0:EC], qkb[:, 0:EC], DH ** -0.5, None, ALU.mult).then_inc(dve_set, 1)
            dve.wait_ge(dve_set, 4)
            dve.wait_ge(consts, 9)

            def moments(x, st, mv, st_sem, mv_sem, n):
                v.bn_stats(st[:, :], x).then_inc(st_sem, 1)
                dve.wait_ge(st_sem, n)
                settled(dve)
                v.bn_aggr(mv[:, :], st[:, :]).then_inc(mv_sem, 1)

            def body(t):
                if t.at:
                    T = GT * t.at[0] + t.at[1]
                if t.dt:
                    TD = GT * t.dt[0] + t.dt[1]
                for step in t.steps:
                    name = step[0]
                    if name == "mx":
                        sm, um = t.mx
                        c, j, h = step[1:]
                        g = keys_groups(sm)
                        i = (c * GT + j) * HJ + h
                        width = (j + 1) * P if c == g - 1 else GQ
                        dve.wait_ge(mx_ready, units_before(sm, um) + i + 1)
                        v.reduce_max(mxs[:, j * HJ + h, c:c + 1], mxbank[i % MXB][:, 0:width], AX_X)\
                            .then_inc(mx_used, 1)
                    elif name == "nm_d":
                        sm, um = t.mx
                        g = keys_groups(sm)
                        job = GT * sm + um
                        dve.wait_ge(mx_used, units_before(sm, um) + units(sm))
                        if g == 1:
                            v.tensor_scalar(nm[:, :], mxs[:, :, 0], -1.0, None, ALU.mult).then_inc(nm_step, 1)
                        else:
                            v.tensor_reduce(nm[:, :], mxs[:, :, 0:g], AX_X, ALU.max, negate=True).then_inc(nm_step, 1)
                        src = nm
                        for a in range(NPART):
                            dve.wait_ge(nm_step, NCHAINM * job + 2 * a + 1)
                            part = nmp[:, :, :, a]
                            srcv = src[:, :].rearrange("p (j h) -> p j h", j=GT)
                            v.tensor_copy(part, srcv).then_inc(nm_step, 1)
                            if a == NPART - 1:
                                break
                            if a == 0:
                                dve.wait_ge(nm_step, NCHAINM * job + 2)
                                v.tensor_tensor(nmd[:, :].rearrange("p (j h) -> p j h", j=GT), srcv, part,
                                                ALU.subtract).then_inc(nm_step, 1)
                                src = nmd
                            else:
                                dve.wait_ge(nm_step, NCHAINM * job + 4)
                                v.tensor_tensor(nmp[:, :, :, 2], srcv, part, ALU.subtract).then_inc(nm_step, 1)
                                break
                    elif name == "o_ctx":
                        sj, hg = t.st
                        job = GT * sj + hg
                        ov = dbank[:, :].rearrange("p (j h x) -> p j h x", j=GT, h=HJ)
                        dve.wait_ge(oT_ps, job + 1)
                        v.reciprocal(oden[:, :, :], ov[:, :, :, DH]).then_inc(oden_ready, 1)
                        dve.wait_ge(oden_ready, job + 1)
                        dst = ctxn[:, (sj % 2) * GT:(sj % 2 + 1) * GT, ds(hg * (HJ * DH), HJ * DH)]\
                            .rearrange("p j (h d) -> p j h d", h=HJ)
                        v.tensor_tensor(dst, ov[:, :, :, 0:DH],
                                        oden[:, :, :].unsqueeze(3).broadcast_to([P, GT, HJ, DH]), ALU.mult)\
                            .then_inc(ctx_ready, 1)
                    elif name == "a_max":
                        dve.wait_ge(sA_ps, T + 1)
                        v.tensor_reduce(nmA[:, :], abank[:, 0:2 * P], AX_X, ALU.max, negate=True)\
                            .then_inc(nmA_ready, 1)
                    elif name == "a_res":
                        dve.wait_ge(pA_ready, T + 1)
                        v.reciprocal(rsA[:, :], sumA[:, :]).then_inc(rsA_ready, 1)
                        dve.wait_ge(rsA_ready, T + 1)
                        dve.wait_ge(oA_ps, T + 1)
                        dve.wait_ge(xb_ready, T + 1)
                        v.scalar_tensor_tensor(out=rA[:, :], in0=abank[:, 0:E], scalar=rsA[:, 0:1], in1=xb[:, :],
                                               op0=ALU.mult, op1=ALU.add).then_inc(rA_ready, 1)
                        dve.wait_ge(rA_ready, T + 1)
                        moments(rA[:, :], stA, mvA, stA_ready, mvA_ready, T + 1)
                    elif name == "a_norm":
                        dve.wait_ge(rstdA_ready, T + 1)
                        dve.wait_ge(mvA_ready, T + 1)
                        if not is_first(T):
                            dve.wait_ge(x0_stored, 16 * T)
                            dve.wait_ge(rxT_ps, T)
                        v.tensor_scalar(x0[:, :], rA[:, :], mvA[:, 0:1], rstdA[:, 0:1], ALU.subtract, ALU.mult)\
                            .then_inc(x0_ready, 1)
                    elif name == "a_qkf":
                        dve.wait_ge(qk_ps, T + 1)
                        if not is_first(T):
                            dve.wait_ge(parts_ready, T)
                        v.tensor_tensor(qkf[:, :, :], abank[:, :].rearrange("p (c t) -> p c t", c=2 * EC),
                                        qkb[:, :].unsqueeze(2).broadcast_to([P, 2 * EC, P]), ALU.add)\
                            .then_inc(qkf_ready, 1)
                    elif name == "a_vst":
                        dve.wait_ge(v_ps, T + 1)
                        if not is_first(T):
                            dve.wait_ge(v_stored, 16 * T)
                        v.tensor_tensor(vst[:, :, 0:DH], abank[:, 0:E].rearrange("p (h d) -> p h d", h=H),
                                        b_v.rearrange("p (h d) -> p h d", h=H), ALU.add).then_inc(vst_ready, 1)
                    elif name == "d_res":
                        dve.wait_ge(oD_ps, TD + 1)
                        dve.wait_ge(x0b_ready, TD + 1)
                        v.tensor_tensor(rD[:, :], dbank[:, 0:E], x0b[:, :], ALU.add).then_inc(rD_ready, 1)
                        dve.wait_ge(rD_ready, 2 * TD + 1)
                        moments(rD[:, :], stD, mvD, stD_ready, mvD_ready, 3 * TD + 1)
                    elif name in ("d_norm", "d_norm2"):
                        k = 1 if name == "d_norm" else 2
                        dve.wait_ge(rstdD_ready, 3 * TD + k)
                        dve.wait_ge(mvD_ready, 3 * TD + k)
                        v.tensor_scalar(xh[:, :], rD[:, :], mvD[:, 0:1], rstdD[:, 0:1], ALU.subtract, ALU.mult)\
                            .then_inc(xh_ready, 1)
                    elif name == "d_lg":
                        if is_first(TD):
                            dve.wait_ge(moe_loaded, 16 * MOE_LOADS)
                        dve.wait_ge(g_ps, TD + 1)
                        v.tensor_tensor(lg[:, :], dbank[:, 0:NE], gb_sb[:, :], ALU.add).then_inc(lg_ready, 1)
                        dve.wait_ge(lg_ready, TD + 1)
                        v.tensor_reduce(ngm[:, :], lg[:, :], AX_X, ALU.max, negate=True).then_inc(ngm_ready, 1)
                    elif name == "d_top":
                        dve.wait_ge(ge_ready, TD + 1)
                        v.reciprocal(gr[:, :], gsum[:, :]).then_inc(top_step, 1)
                        dve.wait_ge(top_step, NTOP * TD + 1)
                        v.tensor_scalar(gates[:, :], ge[:, :], gr[:, 0:1], None, ALU.mult).then_inc(top_step, 1)
                        dve.wait_ge(top_step, NTOP * TD + 2)
                        settled(dve)
                        v.max(top8[:, :], gates[:, :]).then_inc(top_step, 1)
                        dve.wait_ge(top_step, NTOP * TD + 3)
                        settled(dve)
                        v.max_index(ix8[:, :], top8[:, :], gates[:, :]).then_inc(top_step, 1)
                        dve.wait_ge(top_step, NTOP * TD + 4)
                        v.tensor_copy(ixf[:, :], ix8[:, :]).then_inc(top_step, 1)
                        dve.wait_ge(top_step, NTOP * TD + 5)
                        for k, w in enumerate((w1st, w2nd)):
                            v.scalar_tensor_tensor(out=w[:, :], in0=iota8[:, :], scalar=ixf[:, k:k + 1],
                                                   in1=gates[:, :], op0=ALU.is_equal, op1=ALU.mult)\
                                .then_inc(top_step, 1)
                        dve.wait_ge(top_step, NTOP * TD + 7)
                        v.tensor_tensor(wts[:, :], w1st[:, :], w2nd[:, :], ALU.add).then_inc(wts_ready, 1)
                    elif name == "d_acc0":
                        dve.wait_ge(eb_ps, TD + 1)
                        dve.wait_ge(x1_ready, TD + 1)
                        v.tensor_tensor(acc[:, :], dbank[:, 0:E], x1[:, :], ALU.add).then_inc(acc_step, 1)
                    elif name in ("d_e0c", "d_e2c"):
                        k = int(name[3])
                        dve.wait_ge(e_ps, 4 * TD + k + 1)
                        for e in range(2):
                            dve.wait_ge(acc_step, 5 * TD + k + e + 1)
                            v.scalar_tensor_tensor(out=acc[:, :], in0=dbank[:, e * E:(e + 1) * E],
                                                   scalar=wts[:, 2 * k + e:2 * k + e + 1], in1=acc[:, :],
                                                   op0=ALU.mult, op1=ALU.add).then_inc(acc_step, 1)
                    elif name == "d_y":
                        dve.wait_ge(accp_step, 3 * TD + 3)
                        dve.wait_ge(acc_step, 5 * TD + 5)
                        v.tensor_tensor(rD[:, :], acc[:, :], accp[:, :], ALU.add).then_inc(rD_ready, 1)
                        dve.wait_ge(rD_ready, 2 * TD + 2)
                        moments(rD[:, :], stD, mvD, stD_ready, mvD_ready, 3 * TD + 2)
                    elif name == "d_z":
                        dve.wait_ge(z_ready, TD + 1)
                        moments(rD[:, :], stD, mvD, stD_ready, mvD_ready, 3 * TD + 3)
                    elif name == "d_norm3":
                        dve.wait_ge(rstdD_ready, 3 * TD + 3)
                        dve.wait_ge(mvD_ready, 3 * TD + 3)
                        if not is_first(TD):
                            dve.wait_ge(out_stored, 16 * TD)
                        v.tensor_scalar(obuf[:, :], rD[:, :], mvD[:, 0:1], rstdD[:, 0:1], ALU.subtract, ALU.mult)\
                            .then_inc(ob_ready, 1)

            walk(dve, body)

        @block.tensor
        def _(pe):
            mm, tr = nc.tensor.matmul, nc.tensor.transpose
            pe.wait_ge(fold_loaded, 16 * FOLD_LOADS)
            wqkt = pbuf[:, 0:2, :].rearrange("p a b -> p (a b)").rearrange("p (c d) -> p c d", c=2 * EC)
            woutn = pbuf[:, 2, :].rearrange("p (c d) -> p c d", c=EC)
            for k, (lc, rhs) in enumerate(((0, wqkt[:, EC:2 * EC, :]), (EC, woutn))):
                for d in range(EC):
                    for e in range(EC):
                        last = mm(bank[k][:, d * E:(d + 1) * E], wqkt[:, lc + e, d * P:(d + 1) * P], rhs[:, e, :],
                                  start=e == 0, stop=e == EC - 1)
                last.then_inc(fold_ps, 1)
            pe.wait_ge(folded, 2)
            pe.wait_ge(consts, 9)
            pe.wait_ge(dve_set, 4)

            def body(t):
                if t.at:
                    sa, ua = t.at
                    T = GT * sa + ua
                if t.dt:
                    TD = GT * t.dt[0] + t.dt[1]
                for step in t.steps:
                    name = step[0]
                    if name == "mx":
                        sm, um = t.mx
                        c, j, h = step[1:]
                        g = keys_groups(sm)
                        i = (c * GT + j) * HJ + h
                        base = units_before(sm, um)
                        diag = c == g - 1
                        width = (j + 1) * P if diag else GQ
                        if i == 0 and is_first(um):
                            pe.wait_ge(stack_loaded, 16 * 2 * SLOTS * GT * (sm + 1))
                        if not (is_first(base) and i < MXB):
                            pe.wait_ge(mx_used, base + i - MXB + 1)
                        qcol = (um * HJ + h) * (QRING * GQ) + (sm % QRING) * GQ + j * P
                        kcol = (um * HJ + h) * (KRING * GQ) + (((sm // GB) * GB + c) % KRING) * GQ
                        bk = mxbank[i % MXB]
                        last = mm(bk[:, 0:width], qs[0:KR, ds(qcol, P)], ks[0:KR, ds(kcol, width)],
                                  start=True, stop=not diag)
                        if diag:
                            last = mm(bk[:, j * P:(j + 1) * P], idb[:, :], maskb[:, :], start=False, stop=True)
                        last.then_inc(mx_ready, 1)
                    elif name == "nm_T":
                        job = GT * t.mx[0] + t.mx[1]
                        pe.wait_ge(nm_step, NCHAINM * (job + 1))
                        if t.at:
                            pe.wait_ge(vst_ready, T + 1)
                        else:
                            pe.wait_ge(nmT_ready, job)
                        for j in range(GT):
                            last = tr(nmbank[:, j * P:(j + 1) * P],
                                      nmp[:, j, :, :].rearrange("p h a -> p (h a)"), idb[:, :])
                        last.then_inc(nmT_ps, 1)
                    elif name == "st":
                        sj, hg = t.st
                        kb, h = step[1:]
                        i = kb * HJ + h
                        base = units_before(sj, hg)
                        first_diag = key_tiles(sj) - GT
                        r0 = max(0, kb - first_diag) * P
                        if i == 0 and is_first(base):
                            pe.wait_ge(ones_loaded, 16)
                        if i == 0:
                            pe.wait_ge(nm_loaded, 16 * HJ * (GT * sj + hg + 1))
                        if i >= STB:
                            pe.wait_ge(exp_done, base + i - STB + 1)
                        elif not is_first(base):
                            pe.wait_ge(exp_done, base)
                        kcol = (hg * HJ + h) * (KRING * GQ) + (((sj // GB) * GB + kb // GT) % KRING) * GQ + kb % GT * P
                        qcol = (hg * HJ + h) * (QRING * GQ) + (sj % QRING) * GQ + r0
                        bk = stbank[i % STB]
                        last = mm(bk[:, r0:GQ], ks[0:KR + NPART, ds(kcol, P)], qs[0:KR + NPART, ds(qcol, GQ - r0)],
                                  start=True, stop=kb < first_diag)
                        if kb >= first_diag:
                            last = mm(bk[:, r0:r0 + P], maskb[:, :], idb[:, :], start=False, stop=True)
                        last.then_inc(st_ready, 1)
                    elif name == "pv":
                        sj, hg = t.st
                        kb = step[1]
                        last_kb = key_tiles(sj) - 1
                        jj = kb - (last_kb + 1 - GT)
                        r0 = max(0, jj) * P
                        job = GT * sj + hg
                        pe.wait_ge(exp_done, units_before(sj, hg) + HJ * (kb + 1))
                        if kb % GT == 0:
                            pe.wait_ge(vcur_loaded[kb // GT], 16 * (loads_before(sj, hg, kb // GT) + 1))
                        if kb == 0 and not is_first(job):
                            pe.wait_ge(osb_ready, job)
                        for h in range(HJ):
                            last = mm(obank[32 * h:32 * h + DV, r0:GQ], vcur[:, kb, h, :],
                                      pbuf[:, (kb * HJ + h) % PB, r0:GQ], start=kb == 0, stop=kb == last_kb,
                                      tile_position=(0, 32 * h))
                        last.then_inc(pv_done, 1)
                    elif name == "o_T":
                        job = GT * t.st[0] + t.st[1]
                        pe.wait_ge(osb_ready, job + 1)
                        if t.dt:
                            pe.wait_ge(etmp_ready, 2 * (TD + 1))
                        elif not is_first(job):
                            pe.wait_ge(ctx_ready, job)
                        for j in range(GT):
                            last = tr(dbank[:, j * P:(j + 1) * P], osb[:, j * P:(j + 1) * P], idf[:, :])
                        last.then_inc(oT_ps, 1)
                    elif name == "a_xT":
                        pe.wait_ge(xw_loaded, 16 * (T + 1))
                        if t.mx and not is_first(t.mx[1] + GT * t.mx[0]):
                            pe.wait_ge(nmT_ready, GT * t.mx[0] + t.mx[1])
                        elif not is_first(T):
                            pe.wait_ge(vst_ready, T)
                        for c in range(EC):
                            for w in range(2):
                                last = tr(abank[:, (2 * c + w) * P:(2 * c + w + 1) * P], xw[:, w, c * P:(c + 1) * P],
                                          idf[:, :])
                        last.then_inc(xT_ps, 1)
                    elif name == "a_q":
                        pe.wait_ge(xT_ready, T + 1)
                        for co in range(EC):
                            for ci in range(EC):
                                last = mm(abank[:, co * P:(co + 1) * P], m_sb[:, ci, co * P:(co + 1) * P],
                                          xT[:, ci, P:2 * P], start=ci == 0, stop=ci == EC - 1)
                        last.then_inc(qT_ps, 1)
                    elif name == "a_s":
                        pe.wait_ge(qT_ready, T + 1)
                        for c in range(EC):
                            mm(abank[:, 0:2 * P], qT[:, c, :], xT[:, c, :], start=c == 0, stop=False)
                        mm(abank[:, P:2 * P], idb[:, :], maskb[:, :], start=False, stop=True).then_inc(sA_ps, 1)
                    elif name == "a_pT":
                        pe.wait_ge(pA_ready, T + 1)
                        for w in range(2):
                            last = tr(abank[:, w * P:(w + 1) * P], pA[:, w * P:(w + 1) * P], idf[:, :])
                        last.then_inc(pT_ps, 1)
                    elif name == "a_y":
                        pe.wait_ge(pT_ready, T + 1)
                        for c in range(EC):
                            for w in range(2):
                                last = mm(abank[:, c * P:(c + 1) * P], xw[:, w, c * P:(c + 1) * P], pT[:, w, :],
                                          start=w == 0, stop=w == 1)
                        last.then_inc(yT_ps, 1)
                    elif name == "a_o":
                        pe.wait_ge(yT_ready, T + 1)
                        for c in range(EC):
                            last = mm(abank[:, 0:E], yT[:, c, :], wko[:, c, :], start=c == 0, stop=c == EC - 1)
                        last.then_inc(oA_ps, 1)
                    elif name == "a_rT":
                        pe.wait_ge(rp_ready, T + 1)
                        for c in range(2 * EC):
                            src = (rp if c < EC else x0)[:, (c % EC) * P:(c % EC + 1) * P]
                            last = tr(abank[:, c * P:(c + 1) * P], src, idf[:, :])
                        last.then_inc(rxT_ps, 1)
                    elif name == "a_qk":
                        pe.wait_ge(rxT_ready, T + 1)
                        for co in range(2 * EC):
                            for ci in range(EC):
                                last = mm(abank[:, co * P:(co + 1) * P], inw[:, ci, co * P:(co + 1) * P],
                                          rxT[:, ci, :], start=ci == 0, stop=ci == EC - 1)
                        last.then_inc(qk_ps, 1)
                    elif name == "a_v":
                        pe.wait_ge(qkf_ready, T + 1)
                        for ci in range(EC):
                            last = mm(abank[:, 0:E], rxT[:, EC + ci, :], inw[:, ci, 2 * E:3 * E],
                                      start=ci == 0, stop=ci == EC - 1)
                        last.then_inc(v_ps, 1)
                    elif name == "d_cT":
                        pe.wait_ge(cj_ready, TD + 1)
                        if t.st:
                            pe.wait_ge(ctx_ready, GT * t.st[0] + t.st[1])
                        else:
                            pe.wait_ge(ctx_ready, GT * NG)
                            pe.wait_ge(etmp_ready, 2 * TD)
                        for c in range(EC):
                            last = tr(dbank[:, c * P:(c + 1) * P], cj[:, c * P:(c + 1) * P], idf[:, :])
                        last.then_inc(cT_ps, 1)
                    elif name == "d_o":
                        pe.wait_ge(cT_ready, TD + 1)
                        if is_first(TD):
                            pe.wait_ge(moe_loaded, 16 * MOE_LOADS)
                        for c in range(EC):
                            last = mm(dbank[:, 0:E], cT[:, c, :], wo[:, c, :], start=c == 0, stop=c == EC - 1)
                        last.then_inc(oD_ps, 1)
                    elif name == "d_x1T":
                        pe.wait_ge(x1_ready, TD + 1)
                        for c in range(EC):
                            last = tr(dbank[:, c * P:(c + 1) * P], x1[:, c * P:(c + 1) * P], idf[:, :])
                        last.then_inc(x1T_ps, 1)
                    elif name == "d_g":
                        pe.wait_ge(x1T_ready, TD + 1)
                        for c in range(EC):
                            last = mm(dbank[:, 0:NE], x1T[:, c, :], gw[:, c, :], start=c == 0, stop=c == EC - 1)
                        last.then_inc(g_ps, 1)
                    elif name == "d_wT":
                        pe.wait_ge(wts_ready, TD + 1)
                        tr(dbank[0:NE, 0:P], wts[:, :], idf[:, :]).then_inc(wT_ps, 1)
                    elif name == "d_b":
                        pe.wait_ge(wT_ready, TD + 1)
                        mm(dbank[:, 0:E], wT[:, :], eb[:, :], start=True, stop=True).then_inc(eb_ps, 1)
                    elif name in ("d_e0", "d_e1", "d_e2", "d_e3"):
                        k = int(name[3])
                        if k == 0:
                            pe.wait_ge(acc_step, 5 * TD + 1)
                        elif k == 2:
                            pe.wait_ge(etmp_ready, 2 * TD + 1)
                        else:
                            pe.wait_ge(acc_step, 5 * TD + k + 2)
                        for c in range(EC):
                            last = mm(dbank[:, :], x1T[:, c, :], ew[:, c, k * 2 * E:(k + 1) * 2 * E],
                                      start=c == 0, stop=c == EC - 1)
                        last.then_inc(e_ps, 1)

            walk(pe, body)


def kernel(L0_attn_x, L0_attn_w_qkv, L0_attn_w_out, L0_attn_b_out, L0_ffn_in_proj_w, L0_ffn_in_proj_b,
           L0_ffn_out_proj_w, L0_ffn_out_proj_b, L0_ffn_gate_w, L0_ffn_gate_b, L0_ffn_expert_w, L0_ffn_expert_b,
           L0_ffn_ln1_w, L0_ffn_ln1_b, L0_ffn_ln2_w, L0_ffn_ln2_b):
    import concourse.bacc as bacc
    from concourse.bass_utils import run_bass_kernel_spmd as run

    windows = np.zeros((NT + 1, 2, P, E), np.float32)
    tiles = np.asarray(L0_attn_x).reshape(B, TB, P, E)
    windows[:NT, 1] = tiles.reshape(NT, P, E)
    windows[:NT, 0].reshape(B, TB, P, E)[:, 1:] = tiles[:, :-1]
    inv_freq = (1.0 / np.float32(10000.0) ** (np.arange(0, DH, 2, dtype=np.float32) / np.float32(DH)))
    freqs = np.arange(N, dtype=np.float32)[:, None] * inv_freq.astype(np.float32)[None, :]
    cs = np.zeros((N, 2, DH // 2, 2), np.float32)
    cs[:, 0, :, 0] = cs[:, 0, :, 1] = np.cos(freqs)
    cs[:, 1, :, 1] = np.sin(freqs)
    cs[:, 1, :, 0] = -np.sin(freqs)
    rows = np.empty((P, 7, E), np.float32)
    for i, vec in enumerate((L0_attn_b_out, np.asarray(L0_ffn_in_proj_b)[2 * E:], L0_ffn_out_proj_b, L0_ffn_ln1_w,
                             L0_ffn_ln1_b, L0_ffn_ln2_w, L0_ffn_ln2_b)):
        rows[:, i, :] = np.asarray(vec)
    arrays = {
        "windows": windows.reshape((NT + 1) * 2 * P, E),
        "cs": np.concatenate([cs.reshape(N, 2 * DH)] * B + [np.zeros((P, 2 * DH), np.float32)]),
        "w_qk_t": np.asarray(L0_attn_w_qkv)[:, :2 * E].T,
        "w_out": np.asarray(L0_attn_w_out),
        "in_t": np.asarray(L0_ffn_in_proj_w).T,
        "in_b": np.asarray(L0_ffn_in_proj_b)[:2 * E].reshape(2 * EC, P).T,
        "wo_t": np.asarray(L0_ffn_out_proj_w).T,
        "gate_t": np.asarray(L0_ffn_gate_w).T,
        "exp_t": np.asarray(L0_ffn_expert_w).transpose(2, 0, 1).reshape(E, NE * E),
        "exp_b": np.asarray(L0_ffn_expert_b),
        "rows": rows,
        "gate_b": np.broadcast_to(np.asarray(L0_ffn_gate_b)[None, :], (P, NE)),
    }
    arrays = {n: np.ascontiguousarray(a) for n, a in arrays.items()}
    nc = bacc.Bacc("TRN2", target_bir_lowering=False, num_devices=1)
    args = [nc.dram_tensor(n, a.shape, mybir.dt.from_np(a.dtype), kind="ExternalInput").ap()
            for n, a in arrays.items()]
    args.append(nc.dram_tensor("out", (NT * P, E), F32, kind="ExternalOutput").ap())
    build(nc, *args)
    r = run(nc, [arrays], core_ids=[0])
    return r.results[0]["out"].reshape(B, N, E)
```

```python
from contextlib import ExitStack

import numpy as np
import concourse.bass as bass
from concourse import mybir

F32 = mybir.dt.float32
BF16 = mybir.dt.bfloat16
U32 = mybir.dt.uint32
ALU = mybir.AluOpType
ACT = mybir.ActivationFunctionType
AX_X = mybir.AxisListType.X

P = 128
E = 256
EC = E // P
B, N = 2, 2048
H, DH = 16, 16
DV = DH + 1
TB = N // P
NT = B * TB
GT = 4
GQ = GT * P
GB = TB // GT
NG = B * GB
HJ = 4
NE = 8
SLOTS = 6
KR = SLOTS * DH
NPART = 3
Q_PARTS = (0, 0, 0, 1, 1, 2)
K_PARTS = (0, 1, 2, 0, 1, 0)
KRING = GB + 1
QRING = 2
MXB, STB = 2, 3
PB = 8
NEG = -1.0e30
EPS = 1e-5
NCHAINM = 5
NTOP = 7


def ds(start, size):
    return slice(start, start + size) if isinstance(start, int) else bass.ds(start, size)


def is_first(count):
    return isinstance(count, int) and count == 0


def keys_groups(s):
    return s % GB + 1


def units(s):
    return 16 * keys_groups(s)


def units_before(s, hg):
    return sum(HJ * units(x) for x in range(s)) + hg * units(s)


def key_tiles(s):
    return GT * keys_groups(s)


def key_tiles_before(s, hg):
    return sum(HJ * key_tiles(x) for x in range(s)) + hg * key_tiles(s)


def loads_before(s, hg, c):
    return sum(4 for x in range(s) if x % GB >= c) + hg


A_CHAIN = """a_xT a_xTc a_xb a_q a_qc a_s a_max a_exp a_pT a_pTc a_y a_yc a_load a_o a_res a_rstd a_norm
a_st0 a_rope a_load_cs a_rT a_rTc a_qk a_qkf a_v a_vst a_vstore a_split a_pst""".split()
DF_CHAIN = """d_load d_cp f_g f_lg d_xb d_cT d_cTc f_exp d_o f_top d_res d_rstd f_wT f_wTc f_b d_norm f_acc0
f_e0 d_aff f_e0c f_e1 f_e1c f_e1a f_e2 f_e2c f_e3 f_e3c d_x1T d_x1Tc f_e3a f_load f_y f_rstd2 f_norm2 f_aff2
f_z f_rstd3 f_norm3 f_store""".split()


def spread(lists):
    at = []
    for k, (steps, start, end) in enumerate(lists):
        for i, x in enumerate(steps):
            at.append((start + (end - start) * (i + 0.5) / len(steps), k, i, x))
    return [x for _, _, _, x in sorted(at) if x[0] != "."]


def order(mx_s, st_s, has_a, has_stack, has_d, has_f, hold_stack):
    lists = []
    if mx_s is not None:
        g = keys_groups(mx_s)
        lists.append(([("mx", c, j, h) for c in range(g) for j in range(GT) for h in range(HJ)], -0.08, 0.82))
        lists.append(([("nm_d",), ("nm_T",)], 0.80, 1.0))
    if st_s is not None:
        g, st = keys_groups(st_s), []
        for kb in range(GT * g):
            st += [("st", kb, h) for h in range(HJ)]
            if kb:
                st.append(("pv", kb - 1))
                if kb % GT == 0:
                    st.append(("vload", kb // GT - 1))
        st += [("pv", GT * g - 1), ("vload", g - 1)]
        lists.append((st, 0.04, 1.0))
    if has_a:
        lists.append(([(x,) for x in A_CHAIN], -0.08, 0.90))
    df = [(x,) for x in DF_CHAIN if (x[0] == "d" and has_d) or (x[0] == "f" and has_f)]
    if df:
        lists.append((df, -0.08, 0.97))
    steps = [("vload_new",)] + spread(lists)
    if mx_s is not None and has_a:
        assert steps.index(("a_vst",)) < steps.index(("nm_T",))
    if has_stack:
        if hold_stack:
            steps.append(("a_stack",))
        else:
            steps.insert(1, ("a_stack",))
    if st_s is not None:
        steps += [("o_evac",), ("o_T",), ("o_ctx",)]
    return steps


def within(x, limit):
    return 0 <= x < limit


class Turn:

    def __init__(self, s, u0, u):
        n0, first = GT * s + u0, u0 == 0
        self.s, self.u = s, u
        self.mx = (s, u) if within(n0, NT) else None
        self.st = ((s - 1, 3) if first else (s, u - 1)) if within(n0 - 1, NT) else None
        self.at = GT * s + 5 + u if within(n0 + 5, NT) else None
        self.stack = (s + 1, u) if within(n0 + 4, NT) else None
        self.dt = ((s - 2, 3) if first else (s - 1, u - 1)) if within(n0 - 5, NT) else None
        self.ft = (u - 6 + GT * s if isinstance(u, int) else u + (GT * s - 6)) if within(n0 - 6, NT) else None
        self.steps = order(self.mx and s, self.st and self.st[0], self.at is not None, self.stack is not None,
                           self.dt is not None, self.ft is not None, first and s >= 1)

    @staticmethod
    def kind(s, u):
        n = GT * s + u
        return (u == 0, min(max(n, -1), 2), [within(n + k, NT) for k in (5, 4, 0, -1, -5, -6)],
                [n + k == 0 for k in (5, -5, -6)])


def walk(eng, body):
    for s in range(-2, NG + 2):
        u = 0
        while u < GT:
            end = u + 1
            while end < GT and Turn.kind(s, end) == Turn.kind(s, u):
                end += 1
            if -5 <= GT * s + u < NT + 6:
                if end == u + 1:
                    body(Turn(s, u, u))
                else:
                    with eng.Fori(u, end) as reg:
                        body(Turn(s, u, reg))
            u = end


def build(nc, windows, cs, w_qk_t, w_out, in_t, in_b, wo_t, gate_t, exp_t, exp_b, rows, gate_b, out):
    x0_dram = nc.dram_tensor("x0_scratch", (NT * P, E), F32, kind="Internal").ap()
    v_dram = nc.dram_tensor("v_scratch", (NT * P, H * DV), F32, kind="Internal").ap()
    parts_dram = nc.dram_tensor("parts_scratch", (NT * NPART * 2 * E, P), BF16, kind="Internal").ap()

    with ExitStack() as ctx:
        def sb(name, shape, dt=F32):
            return ctx.enter_context(nc.sbuf_tensor(name, shape, dt))

        def sem(name):
            return ctx.enter_context(nc.semaphore(name))

        idf = sb("idf", [P, P])
        idb = sb("idb", [P, P], BF16)
        maskb = sb("maskb", [P, P], BF16)
        iota8 = sb("iota8", [P, NE])
        mhalf = sb("mhalf", [P, 1])
        m_sb = sb("m_sb", [P, EC, E])
        wko = sb("wko", [P, EC, E])
        inw = sb("inw", [P, EC, 3 * E])
        wo = sb("wo", [P, EC, E])
        gw = sb("gw", [P, EC, NE])
        ew = sb("ew", [P, EC, NE * E])
        eb = sb("eb", [NE, E])
        qkb = sb("qkb", [P, 2 * EC])
        rowv = sb("rowv", [P, 7, E])
        gb_sb = sb("gb_sb", [P, NE])
        b_out, b_v, b_op, g1, b1, g2, b2 = (rowv[:, i, :] for i in range(7))

        qs = sb("qs", [P, H * QRING * GQ], BF16)
        ks = sb("ks", [P, H * KRING * GQ], BF16)
        qs3 = qs[:, :].rearrange("p (h c) -> p h c", h=H)
        ks3 = ks[:, :].rearrange("p (h c) -> p h c", h=H)
        vcur = sb("vcur", [P, TB, HJ, DV])
        pbuf = sb("pbuf", [P, PB, GQ])
        mxs = sb("mxs", [P, GT * HJ, GB])
        nm = sb("nm", [P, GT * HJ])
        nmd = sb("nmd", [P, GT * HJ])
        nmp = sb("nmp", [P, GT, HJ, NPART], BF16)
        nmT = sb("nmT", [NPART * HJ, GQ], BF16)
        osb = sb("osb", [P, GQ])
        oden = sb("oden", [P, GT, HJ])
        ctxn = sb("ctxn", [P, 2 * GT, E])

        xw = sb("xw", [P, 2, E])
        cst = sb("cst", [P, 2, DH])
        xb = sb("xb", [P, E])
        xT = sb("xT", [P, EC, 2 * P])
        qT = sb("qT", [P, EC, P])
        nmA = sb("nmA", [P, 1])
        sumA = sb("sumA", [P, 1])
        rsA = sb("rsA", [P, 1])
        pA = sb("pA", [P, 2 * P])
        pT = pA[:, :].rearrange("p (w t) -> p w t", w=2)
        yT = qT
        rA = xb
        stA = sb("stA", [P, 6])
        mvA = sb("mvA", [P, 2])
        veA = sb("veA", [P, 1])
        rstdA = sb("rstdA", [P, 1])
        x0 = sb("x0", [P, E])
        rp = pA
        rxT = xT[:, :, :].rearrange("p c (w t) -> p (c w) t", w=2)
        qkf = sb("qkf", [P, 2 * EC, P])
        qkr = sb("qkr", [P, 2 * EC, P])
        rps = qkr[:, 0:2, :].rearrange("p c t -> p (c t)")
        parts = sb("parts", [P, NPART, 2 * EC, P], BF16)
        vst = sb("vst", [P, H, DV])

        x0b = sb("x0b", [P, E])
        cj = sb("cj", [P, E])
        cT = sb("cT", [P, EC, P])
        rD = sb("rD", [P, E])
        stD = sb("stD", [P, 6])
        mvD = sb("mvD", [P, 2])
        veD = sb("veD", [P, 1])
        rstdD = sb("rstdD", [P, 1])
        x1 = sb("x1", [P, E])
        x1T = sb("x1T", [P, EC, P])

        lg = sb("lg", [P, NE])
        ngm = sb("ngm", [P, 1])
        ge = sb("ge", [P, NE])
        gsum = sb("gsum", [P, 1])
        gr = sb("gr", [P, 1])
        gates = sb("gates", [P, NE])
        top8 = sb("top8", [P, 8])
        ix8 = sb("ix8", [P, 8], U32)
        ixf = sb("ixf", [P, 8])
        w1st = sb("w1st", [P, NE])
        w2nd = sb("w2nd", [P, NE])
        wts = sb("wts", [P, NE])
        wT = sb("wT", [NE, P])
        acc = sb("acc", [P, E])
        etmp = sb("etmp", [P, 2, E])
        xh2, x0f = etmp[:, 0, :], etmp[:, 1, :]
        accp = cj
        stF = sb("stF", [P, 6])
        mvF = sb("mvF", [P, 2])
        veF = sb("veF", [P, 1])
        rstdF = sb("rstdF", [P, 1])

        bank = [ctx.enter_context(nc.psum_tensor(f"bank{i}", [P, 512], F32)) for i in range(8)]
        mxbank, stbank, obank, abank, dbank = bank[0:MXB], bank[MXB:MXB + STB], bank[5], bank[6], bank[7]
        nmbank = abank[0:NPART * HJ, 0:GQ // 2].bitcast(BF16)

        fold_loaded = sem("fold_loaded")
        proj_loaded = sem("proj_loaded")
        moe_loaded = sem("moe_loaded")
        ones_loaded = sem("ones_loaded")
        consts = sem("consts")
        fold_ps = sem("fold_ps")
        folded = sem("folded")
        dve_set = sem("dve_set")
        mx_ready = sem("mx_ready")
        mx_used = sem("mx_used")
        nm_step = sem("nm_step")
        nmT_ps = sem("nmT_ps")
        nmT_ready = sem("nmT_ready")
        nm_loaded = sem("nm_loaded")
        st_ready = sem("st_ready")
        exp_done = sem("exp_done")
        pv_done = sem("pv_done")
        vcur_loaded = [sem(f"vcur_loaded{c}") for c in range(GB)]
        osb_ready = sem("osb_ready")
        oT_ps = sem("oT_ps")
        oden_ready = sem("oden_ready")
        ctx_ready = sem("ctx_ready")
        xw_loaded = sem("xw_loaded")
        cs_loaded = sem("cs_loaded")
        xT_ps = sem("xT_ps")
        xT_ready = sem("xT_ready")
        xb_ready = sem("xb_ready")
        qT_ps = sem("qT_ps")
        qT_ready = sem("qT_ready")
        sA_ps = sem("sA_ps")
        nmA_ready = sem("nmA_ready")
        pA_ready = sem("pA_ready")
        pT_ps = sem("pT_ps")
        pT_ready = sem("pT_ready")
        yT_ps = sem("yT_ps")
        yT_ready = sem("yT_ready")
        oA_ps = sem("oA_ps")
        rsA_ready = sem("rsA_ready")
        rA_ready = sem("rA_ready")
        stA_ready = sem("stA_ready")
        mvA_ready = sem("mvA_ready")
        veA_ready = sem("veA_ready")
        rstdA_ready = sem("rstdA_ready")
        x0_ready = sem("x0_ready")
        x0_stored = sem("x0_stored")
        rope_step = sem("rope_step")
        rp_ready = sem("rp_ready")
        rxT_ps = sem("rxT_ps")
        rxT_ready = sem("rxT_ready")
        qk_ps = sem("qk_ps")
        qkf_ready = sem("qkf_ready")
        v_ps = sem("v_ps")
        vst_ready = sem("vst_ready")
        v_stored = sem("v_stored")
        split_step = sem("split_step")
        parts_ready = sem("parts_ready")
        parts_stored = sem("parts_stored")
        stack_loaded = sem("stack_loaded")
        x0b_loaded = sem("x0b_loaded")
        cj_ready = sem("cj_ready")
        cT_ps = sem("cT_ps")
        cT_ready = sem("cT_ready")
        x0b_ready = sem("x0b_ready")
        oD_ps = sem("oD_ps")
        rD_ready = sem("rD_ready")
        stD_ready = sem("stD_ready")
        mvD_ready = sem("mvD_ready")
        veD_ready = sem("veD_ready")
        rstdD_ready = sem("rstdD_ready")
        xh_ready = sem("xh_ready")
        aff_step = sem("aff_step")
        x1_ready = sem("x1_ready")
        x1T_ps = sem("x1T_ps")
        x1T_ready = sem("x1T_ready")
        g_ps = sem("g_ps")
        lg_ready = sem("lg_ready")
        ngm_ready = sem("ngm_ready")
        ge_ready = sem("ge_ready")
        top_step = sem("top_step")
        wts_ready = sem("wts_ready")
        wT_ps = sem("wT_ps")
        wT_ready = sem("wT_ready")
        eb_ps = sem("eb_ps")
        acc_step = sem("acc_step")
        e_ps = sem("e_ps")
        etmp_ready = sem("etmp_ready")
        accp_step = sem("accp_step")
        y_ready = sem("y_ready")
        stF_ready = sem("stF_ready")
        mvF_ready = sem("mvF_ready")
        veF_ready = sem("veF_ready")
        rstdF_ready = sem("rstdF_ready")
        xh2_ready = sem("xh2_ready")
        aff2_step = sem("aff2_step")
        x0f_loaded = sem("x0f_loaded")
        z_ready = sem("z_ready")
        ob_ready = sem("ob_ready")
        out_stored = sem("out_stored")

        waited = {e.engine: sem(f"waited_{i}") for i, e in enumerate((nc.sync, nc.gpsimd, nc.vector))}
        FOLD_LOADS, PROJ_LOADS, MOE_LOADS = 2, 3, 6

        def settled(eng):
            eng.sem_inc(waited[eng.engine], 1)

        block = ctx.enter_context(nc.Block())

        @block.sync
        def _(sp):
            wqkt = pbuf[:, 0:2, :].rearrange("p a b -> p (a b)").rearrange("p (c d) -> p c d", c=2 * EC)
            woutn = pbuf[:, 2, :].rearrange("p (c d) -> p c d", c=EC)

            def load_windows(T):
                sp.dma_start(xw[:, :, :], windows[ds(T * (2 * P), 2 * P), :].rearrange("(w p) d -> p w d", p=P))\
                    .then_inc(xw_loaded, 16)

            def load_angles(T):
                sp.dma_start(cst[:, :, :].rearrange("p k i -> p (k i)"), cs[ds(T * P, P), :]).then_inc(cs_loaded, 16)

            for dst, src in ((wqkt, w_qk_t.rearrange("(c p) d -> p c d", p=P)),
                             (woutn, w_out.rearrange("(c p) d -> p c d", p=P))):
                sp.dma_start(dst, src).then_inc(fold_loaded, 16)
            load_windows(0)
            for dst, src in ((inw[:, :, :], in_t.rearrange("(c p) d -> p c d", p=P)), (qkb[:, :], in_b),
                             (rowv[:, :, :], rows)):
                sp.dma_start(dst, src).then_inc(proj_loaded, 16)
            load_angles(0)
            sp.wait_ge(dve_set, 2)
            sp.dma_start(ks3[KR:KR + NPART, 1:H, :],
                         ks3[KR:KR + NPART, 0:1, :].broadcast_to([NPART, H - 1, KRING * GQ])).then_inc(ones_loaded, 16)
            for dst, src in (
                (wo[:, :, :], wo_t.rearrange("(c p) d -> p c d", p=P)),
                (gw[:, :, :], gate_t.rearrange("(c p) d -> p c d", p=P)),
                (gb_sb[:, :], gate_b),
                (eb[:, :], exp_b),
                (ew[:, 0, :], exp_t[0:P, :]),
                (ew[:, 1, :], exp_t[P:2 * P, :]),
            ):
                sp.dma_start(dst, src).then_inc(moe_loaded, 16)

            def body(t):
                T, TF = t.at, t.ft
                if t.dt:
                    TD = GT * t.dt[0] + t.dt[1]
                for step in t.steps:
                    name = step[0]
                    if name == "a_load":
                        sp.wait_ge(xb_ready, T + 1)
                        sp.wait_ge(yT_ps, T + 1)
                        load_windows(T + 1)
                    elif name == "a_load_cs":
                        sp.wait_ge(rp_ready, T + 1)
                        load_angles(T + 1)
                    elif name == "a_st0":
                        sp.wait_ge(x0_ready, T + 1)
                        sp.dma_start(x0_dram[ds(T * P, P), :], x0[:, :]).then_inc(x0_stored, 16)
                    elif name == "a_vstore":
                        sp.wait_ge(vst_ready, T + 1)
                        sp.dma_start(v_dram[ds(T * P, P), :], vst[:, :, :].rearrange("p h d -> p (h d)"))\
                            .then_inc(v_stored, 16)
                    elif name == "a_pst":
                        sp.wait_ge(parts_ready, T + 1)
                        sp.dma_start(parts_dram[ds(T * (NPART * 2 * E), NPART * 2 * E), :]
                                     .rearrange("(x p) t -> p x t", p=P),
                                     parts[:, :, :, :].rearrange("p a c t -> p (a c) t")).then_inc(parts_stored, 16)
                    elif name == "a_stack":
                        sa, ua = t.stack
                        TS = GT * sa + ua
                        sp.wait_ge(parts_stored, 16 * (TS + 1))
                        if is_first(ua) and sa >= 2:
                            sp.wait_ge(pv_done, key_tiles_before(sa - 1, 0))
                        for q, (dst, ring, a_of) in enumerate(((qs3, QRING, Q_PARTS), (ks3, KRING, K_PARTS))):
                            col = (sa % ring) * GQ + ua * P
                            for slot, a in enumerate(a_of):
                                r0 = TS * (NPART * 2 * E) + (a * 2 + q) * E
                                sp.dma_start(dst[slot * DH:(slot + 1) * DH, :, ds(col, P)],
                                             parts_dram[ds(r0, E), :].rearrange("(h d) t -> d h t", d=DH))\
                                    .then_inc(stack_loaded, 16)
                    elif name in ("vload_new", "vload"):
                        if not t.mx:
                            continue
                        sm, um = t.mx
                        held = keys_groups(t.st[0]) if t.st else 0
                        if name == "vload_new":
                            if is_first(um):
                                sp.wait_ge(v_stored, 16 * GT * (sm + 1))
                            if t.st and held < keys_groups(sm):
                                sp.wait_ge(pv_done, key_tiles_before(*t.st))
                            chunks = range(held, keys_groups(sm))
                        else:
                            c = step[1]
                            chunks = [c] if c < keys_groups(sm) else []
                            if chunks:
                                sp.wait_ge(pv_done, key_tiles_before(*t.st) + GT * (c + 1))
                        for c in chunks:
                            r0 = ((sm // GB) * TB + c * GT) * P
                            sp.dma_start(vcur[:, GT * c:GT * (c + 1), :, :].rearrange("p k h d -> p k (h d)"),
                                         v_dram[r0:r0 + GT * P, ds(um * (HJ * DV), HJ * DV)]
                                         .rearrange("(k p) x -> p k x", p=P)).then_inc(vcur_loaded[c], 16)
                    elif name == "nm_T":
                        sm, um = t.mx
                        sp.wait_ge(nmT_ready, GT * sm + um + 1)
                        for h in range(HJ):
                            sp.dma_start(qs[KR:KR + NPART, ds((um * HJ + h) * (QRING * GQ) + (sm % QRING) * GQ, GQ)],
                                         nmT[h * NPART:(h + 1) * NPART, :]).then_inc(nm_loaded, 16)
                    elif name == "d_load":
                        sp.wait_ge(x0_stored, 16 * (TD + 1))
                        settled(sp)
                        if not is_first(TD):
                            sp.wait_ge(rD_ready, TD)
                        sp.dma_start(x0b[:, :], x0_dram[ds(TD * P, P), :]).then_inc(x0b_loaded, 16)
                    elif name == "f_load":
                        sp.wait_ge(accp_step, 3 * TF + 3)
                        sp.dma_start(x0f, x0_dram[ds(TF * P, P), :]).then_inc(x0f_loaded, 16)
                    elif name == "f_store":
                        sp.wait_ge(ob_ready, TF + 1)
                        sp.dma_start(out[ds(TF * P, P), :], acc[:, :]).then_inc(out_stored, 16)

            walk(sp, body)
            sp.wait_ge(xw_loaded, 16 * (NT + 1))
            sp.wait_ge(cs_loaded, 16 * (NT + 1))
            sp.wait_ge(x0_stored, 16 * NT)
            sp.wait_ge(v_stored, 16 * NT)
            sp.wait_ge(parts_stored, 16 * NT)
            sp.wait_ge(out_stored, 16 * NT)

        @block.gpsimd
        def _(pool):
            pool.memset(idf[:, :], 0.0).then_inc(consts, 1)
            pool.memset(idb[:, :], 0.0).then_inc(consts, 1)
            pool.memset(maskb[:, :], 0.0).then_inc(consts, 1)
            pool.memset(mhalf[:, :], -0.5).then_inc(consts, 1)
            pool.memset(vst[:, :, :], 1.0).then_inc(consts, 1)
            pool.iota(iota8[:, :], pattern=[[1, NE]], base=0, channel_multiplier=0,
                      allow_small_or_imprecise_dtypes=True).then_inc(consts, 1)
            pool.wait_ge(consts, 6)
            for m in (idf, idb):
                pool.affine_select(out=m[:, :], in_=m[:, :], compare_op=ALU.not_equal, fill=1.0, base=0,
                                   pattern=[[-1, P]], channel_multiplier=1).then_inc(consts, 1)
            pool.affine_select(out=maskb[:, :], in_=maskb[:, :], compare_op=ALU.is_ge, fill=NEG, base=0,
                               pattern=[[-1, P]], channel_multiplier=1).then_inc(consts, 1)
            pool.wait_ge(proj_loaded, 16 * PROJ_LOADS)

            def body(t):
                T, TF = t.at, t.ft
                if t.dt:
                    sd, ud = t.dt
                    TD = GT * sd + ud
                for step in t.steps:
                    name = step[0]
                    if name == "a_xb":
                        pool.wait_ge(xw_loaded, 16 * (T + 1))
                        if not is_first(T):
                            pool.wait_ge(x0_ready, T)
                        pool.tensor_tensor(xb[:, :], xw[:, 1, :], b_out, ALU.add).then_inc(xb_ready, 1)
                    elif name == "a_rstd":
                        pool.wait_ge(mvA_ready, T + 1)
                        settled(pool)
                        pool.tensor_scalar(veA[:, :], mvA[:, 1:2], EPS, None, ALU.add).then_inc(veA_ready, 1)
                        pool.wait_ge(veA_ready, T + 1)
                        pool.tensor_tensor(rstdA[:, :], veA[:, :], mhalf[:, :], ALU.pow).then_inc(rstdA_ready, 1)
                    elif name == "a_rope":
                        pool.wait_ge(x0_ready, T + 1)
                        pool.wait_ge(cs_loaded, 16 * (T + 1))
                        if not is_first(T):
                            pool.wait_ge(rxT_ps, T)
                        xv = x0[:, :].rearrange("p (h i e) -> p h i e", h=H, e=2)
                        cosv = cst[:, 0, :].unsqueeze(1).broadcast_to([P, H, DH])
                        sv = cst[:, 1, :].rearrange("p (i e) -> p i e", e=2)
                        rsv = rps.rearrange("p (h i e) -> p h i e", h=H, e=2)
                        pool.tensor_tensor(rp[:, :].rearrange("p (h i) -> p h i", h=H),
                                           x0[:, :].rearrange("p (h i) -> p h i", h=H), cosv, ALU.mult)\
                            .then_inc(rope_step, 1)
                        for e in range(2):
                            pool.tensor_tensor(rsv[:, :, :, e], xv[:, :, :, 1 - e],
                                               sv[:, :, e].unsqueeze(1).broadcast_to([P, H, DH // 2]), ALU.mult)\
                                .then_inc(rope_step, 1)
                        pool.wait_ge(rope_step, 3 * (T + 1))
                        pool.tensor_tensor(rp[:, :], rp[:, :], rps, ALU.add).then_inc(rp_ready, 1)
                    elif name == "a_split":
                        pool.wait_ge(qkf_ready, T + 1)
                        if not is_first(T):
                            pool.wait_ge(parts_stored, 16 * T)
                        settled(pool)
                        pool.tensor_copy(parts[:, 0, :, :], qkf[:, :, :]).then_inc(split_step, 1)
                        pool.wait_ge(split_step, 3 * T + 1)
                        pool.tensor_tensor(qkr[:, :, :], qkf[:, :, :], parts[:, 0, :, :], ALU.subtract)\
                            .then_inc(split_step, 1)
                        pool.wait_ge(split_step, 3 * T + 2)
                        settled(pool)
                        pool.tensor_copy(parts[:, 1, :, :], qkr[:, :, :]).then_inc(split_step, 1)
                        pool.wait_ge(split_step, 3 * T + 3)
                        pool.tensor_tensor(parts[:, 2, :, :], qkr[:, :, :], parts[:, 1, :, :], ALU.subtract)\
                            .then_inc(parts_ready, 1)
                    elif name == "d_cp":
                        sd, ud = t.dt
                        pool.wait_ge(ctx_ready, GT * (sd + 1))
                        if is_first(TD - 1):
                            pool.wait_ge(cT_ps, TD)
                        elif not is_first(TD):
                            pool.wait_ge(y_ready, TD - 1)
                        settled(pool)
                        pool.tensor_copy(cj[:, :], ctxn[:, ds((sd % 2) * GT + ud, 1), :]
                                         .rearrange("p a b -> p (a b)")).then_inc(cj_ready, 1)
                    elif name == "d_xb":
                        pool.wait_ge(x0b_loaded, 16 * (TD + 1))
                        pool.tensor_tensor(x0b[:, :], x0b[:, :], b_op, ALU.add).then_inc(x0b_ready, 1)
                    elif name == "d_rstd":
                        pool.wait_ge(mvD_ready, TD + 1)
                        settled(pool)
                        pool.tensor_scalar(veD[:, :], mvD[:, 1:2], EPS, None, ALU.add).then_inc(veD_ready, 1)
                        pool.wait_ge(veD_ready, TD + 1)
                        pool.tensor_tensor(rstdD[:, :], veD[:, :], mhalf[:, :], ALU.pow).then_inc(rstdD_ready, 1)
                    elif name in ("f_rstd2", "f_rstd3"):
                        k = int(name[-1]) - 1
                        pool.wait_ge(mvF_ready, 2 * TF + k)
                        settled(pool)
                        pool.tensor_scalar(veF[:, :], mvF[:, 1:2], EPS, None, ALU.add).then_inc(veF_ready, 1)
                        pool.wait_ge(veF_ready, 2 * TF + k)
                        pool.tensor_tensor(rstdF[:, :], veF[:, :], mhalf[:, :], ALU.pow).then_inc(rstdF_ready, 1)
                    elif name == "d_aff":
                        pool.wait_ge(xh_ready, TD + 1)
                        pool.tensor_tensor(rD[:, :], rD[:, :], g1, ALU.mult).then_inc(aff_step, 1)
                        pool.wait_ge(aff_step, TD + 1)
                        if not is_first(TD):
                            pool.wait_ge(acc_step, 5 * TD - 4)
                        pool.tensor_tensor(x1[:, :], rD[:, :], b1, ALU.add).then_inc(x1_ready, 1)
                    elif name == "f_e1a":
                        pool.wait_ge(etmp_ready, 2 * TF + 1)
                        if t.dt:
                            pool.wait_ge(cT_ps, TD + 1)
                        pool.tensor_tensor(accp[:, :], etmp[:, 0, :], etmp[:, 1, :], ALU.add).then_inc(accp_step, 1)
                    elif name == "f_e3a":
                        pool.wait_ge(etmp_ready, 2 * TF + 2)
                        pool.wait_ge(accp_step, 3 * TF + 1)
                        pool.tensor_tensor(accp[:, :], accp[:, :], etmp[:, 0, :], ALU.add).then_inc(accp_step, 1)
                        pool.wait_ge(accp_step, 3 * TF + 2)
                        pool.tensor_tensor(accp[:, :], accp[:, :], etmp[:, 1, :], ALU.add).then_inc(accp_step, 1)
                    elif name == "f_aff2":
                        pool.wait_ge(xh2_ready, TF + 1)
                        pool.tensor_tensor(xh2, xh2, g2, ALU.mult).then_inc(aff2_step, 1)
                        pool.wait_ge(aff2_step, 2 * TF + 1)
                        pool.tensor_tensor(xh2, xh2, b2, ALU.add).then_inc(aff2_step, 1)
                        pool.wait_ge(aff2_step, 2 * TF + 2)
                        pool.wait_ge(x0f_loaded, 16 * (TF + 1))
                        pool.tensor_tensor(acc[:, :], xh2, x0f, ALU.add).then_inc(z_ready, 1)

            walk(pool, body)

        @block.scalar
        def _(act):
            def copy(o, i, scale=1.0):
                return nc.scalar.activation(o, i, ACT.Copy, scale=scale)

            for k, w in enumerate((m_sb, wko)):
                act.wait_ge(fold_ps, k + 1)
                copy(w[:, :, :], bank[k][:, :].rearrange("p (c d) -> p c d", c=EC)).then_inc(folded, 1)

            def body(t):
                T, TF = t.at, t.ft
                if t.dt:
                    TD = GT * t.dt[0] + t.dt[1]
                for step in t.steps:
                    name = step[0]
                    if name == "st":
                        sj, hg = t.st
                        kb, h = step[1:]
                        i = kb * HJ + h
                        base = units_before(sj, hg)
                        r0 = max(0, kb - (key_tiles(sj) - GT)) * P
                        act.wait_ge(st_ready, base + i + 1)
                        if h == 0 and not (is_first(base) and kb < 2):
                            act.wait_ge(pv_done, key_tiles_before(sj, hg) + kb - 1)
                        nc.scalar.activation(pbuf[:, i % PB, r0:GQ], stbank[i % STB][:, r0:GQ], ACT.Exp)\
                            .then_inc(exp_done, 1)
                    elif name == "nm_T":
                        job = GT * t.mx[0] + t.mx[1]
                        act.wait_ge(nmT_ps, job + 1)
                        if not is_first(job):
                            act.wait_ge(nm_loaded, 16 * HJ * job)
                        copy(nmT[:, :], nmbank).then_inc(nmT_ready, 1)
                    elif name == "o_evac":
                        act.wait_ge(pv_done, key_tiles_before(*t.st) + key_tiles(t.st[0]))
                        copy(osb[:, :], obank[:, :]).then_inc(osb_ready, 1)
                    elif name == "a_xTc":
                        act.wait_ge(xT_ps, T + 1)
                        copy(xT[:, :, :], abank[:, :].rearrange("p (c t) -> p c t", c=EC)).then_inc(xT_ready, 1)
                    elif name == "a_qc":
                        act.wait_ge(qT_ps, T + 1)
                        copy(qT[:, :, :], abank[:, 0:E].rearrange("p (c t) -> p c t", c=EC), E ** -0.5)\
                            .then_inc(qT_ready, 1)
                    elif name == "a_exp":
                        act.wait_ge(nmA_ready, T + 1)
                        nc.scalar.activation(pA[:, :], abank[:, 0:2 * P], ACT.Exp, bias=nmA[:, 0:1],
                                             accum_out=sumA[:, 0:1]).then_inc(pA_ready, 1)
                    elif name == "a_pTc":
                        act.wait_ge(pT_ps, T + 1)
                        copy(pT, abank[:, 0:2 * P].rearrange("p (c t) -> p c t", c=2)).then_inc(pT_ready, 1)
                    elif name == "a_yc":
                        act.wait_ge(yT_ps, T + 1)
                        copy(yT[:, :, :], abank[:, 0:E].rearrange("p (c t) -> p c t", c=EC)).then_inc(yT_ready, 1)
                    elif name == "a_rTc":
                        act.wait_ge(rxT_ps, T + 1)
                        copy(rxT, abank[:, :].rearrange("p (c t) -> p c t", c=2 * EC)).then_inc(rxT_ready, 1)
                    elif name == "d_cTc":
                        act.wait_ge(cT_ps, TD + 1)
                        copy(cT[:, :, :], dbank[:, 0:E].rearrange("p (c t) -> p c t", c=EC)).then_inc(cT_ready, 1)
                    elif name == "d_x1Tc":
                        act.wait_ge(x1T_ps, TD + 1)
                        copy(x1T[:, :, :], dbank[:, 0:E].rearrange("p (c t) -> p c t", c=EC)).then_inc(x1T_ready, 1)
                    elif name == "f_exp":
                        act.wait_ge(ngm_ready, TF + 1)
                        nc.scalar.activation(ge[:, :], lg[:, :], ACT.Exp, bias=ngm[:, 0:1], accum_out=gsum[:, 0:1])\
                            .then_inc(ge_ready, 1)
                    elif name == "f_wTc":
                        act.wait_ge(wT_ps, TF + 1)
                        copy(wT[:, :], dbank[0:NE, 0:P]).then_inc(wT_ready, 1)
                    elif name in ("f_e1c", "f_e3c"):
                        k = int(name[3])
                        act.wait_ge(e_ps, 4 * TF + k + 1)
                        if name == "f_e3c":
                            act.wait_ge(accp_step, 3 * TF + 1)
                        elif not is_first(TF):
                            act.wait_ge(z_ready, TF)
                        copy(etmp[:, 0, :], dbank[:, 0:E], wts[:, 2 * k:2 * k + 1])
                        copy(etmp[:, 1, :], dbank[:, E:2 * E], wts[:, 2 * k + 1:2 * k + 2]).then_inc(etmp_ready, 1)

            walk(act, body)

        @block.vector
        def _(dve):
            v = nc.vector
            v.memset(obank[:, :], 0.0).then_inc(dve_set, 1)
            v.memset(ks3[KR:KR + NPART, 0, :], 1.0).then_inc(dve_set, 1)
            dve.wait_ge(proj_loaded, 16 * PROJ_LOADS)
            v.tensor_scalar(inw[:, :, 0:E], inw[:, :, 0:E], DH ** -0.5, None, ALU.mult).then_inc(dve_set, 1)
            v.tensor_scalar(qkb[:, 0:EC], qkb[:, 0:EC], DH ** -0.5, None, ALU.mult).then_inc(dve_set, 1)
            dve.wait_ge(dve_set, 4)
            dve.wait_ge(consts, 9)

            def moments(x, st, mv, st_sem, mv_sem, n):
                v.bn_stats(st[:, :], x).then_inc(st_sem, 1)
                dve.wait_ge(st_sem, n)
                settled(dve)
                v.bn_aggr(mv[:, :], st[:, :]).then_inc(mv_sem, 1)

            def body(t):
                T, TF = t.at, t.ft
                if t.dt:
                    TD = GT * t.dt[0] + t.dt[1]
                for step in t.steps:
                    name = step[0]
                    if name == "mx":
                        sm, um = t.mx
                        c, j, h = step[1:]
                        g = keys_groups(sm)
                        i = (c * GT + j) * HJ + h
                        width = (j + 1) * P if c == g - 1 else GQ
                        dve.wait_ge(mx_ready, units_before(sm, um) + i + 1)
                        v.reduce_max(mxs[:, j * HJ + h, c:c + 1], mxbank[i % MXB][:, 0:width], AX_X)\
                            .then_inc(mx_used, 1)
                    elif name == "nm_d":
                        sm, um = t.mx
                        g = keys_groups(sm)
                        job = GT * sm + um
                        dve.wait_ge(mx_used, units_before(sm, um) + units(sm))
                        if g == 1:
                            v.tensor_scalar(nm[:, :], mxs[:, :, 0], -1.0, None, ALU.mult).then_inc(nm_step, 1)
                        else:
                            v.tensor_reduce(nm[:, :], mxs[:, :, 0:g], AX_X, ALU.max, negate=True).then_inc(nm_step, 1)
                        src = nm
                        for a in range(NPART):
                            dve.wait_ge(nm_step, NCHAINM * job + 2 * a + 1)
                            part = nmp[:, :, :, a]
                            srcv = src[:, :].rearrange("p (j h) -> p j h", j=GT)
                            v.tensor_copy(part, srcv).then_inc(nm_step, 1)
                            if a == NPART - 1:
                                break
                            if a == 0:
                                dve.wait_ge(nm_step, NCHAINM * job + 2)
                                v.tensor_tensor(nmd[:, :].rearrange("p (j h) -> p j h", j=GT), srcv, part,
                                                ALU.subtract).then_inc(nm_step, 1)
                                src = nmd
                            else:
                                dve.wait_ge(nm_step, NCHAINM * job + 4)
                                v.tensor_tensor(nmp[:, :, :, 2], srcv, part, ALU.subtract).then_inc(nm_step, 1)
                                break
                    elif name == "o_ctx":
                        sj, hg = t.st
                        job = GT * sj + hg
                        ov = dbank[:, :].rearrange("p (j h x) -> p j h x", j=GT, h=HJ)
                        dve.wait_ge(oT_ps, job + 1)
                        v.reciprocal(oden[:, :, :], ov[:, :, :, DH]).then_inc(oden_ready, 1)
                        dve.wait_ge(oden_ready, job + 1)
                        dst = ctxn[:, (sj % 2) * GT:(sj % 2 + 1) * GT, ds(hg * (HJ * DH), HJ * DH)]\
                            .rearrange("p j (h d) -> p j h d", h=HJ)
                        v.tensor_tensor(dst, ov[:, :, :, 0:DH],
                                        oden[:, :, :].unsqueeze(3).broadcast_to([P, GT, HJ, DH]), ALU.mult)\
                            .then_inc(ctx_ready, 1)
                    elif name == "a_max":
                        dve.wait_ge(sA_ps, T + 1)
                        v.tensor_reduce(nmA[:, :], abank[:, 0:2 * P], AX_X, ALU.max, negate=True)\
                            .then_inc(nmA_ready, 1)
                    elif name == "a_res":
                        dve.wait_ge(pA_ready, T + 1)
                        v.reciprocal(rsA[:, :], sumA[:, :]).then_inc(rsA_ready, 1)
                        dve.wait_ge(rsA_ready, T + 1)
                        dve.wait_ge(oA_ps, T + 1)
                        dve.wait_ge(xb_ready, T + 1)
                        v.scalar_tensor_tensor(out=rA[:, :], in0=abank[:, 0:E], scalar=rsA[:, 0:1], in1=xb[:, :],
                                               op0=ALU.mult, op1=ALU.add).then_inc(rA_ready, 1)
                        dve.wait_ge(rA_ready, T + 1)
                        moments(rA[:, :], stA, mvA, stA_ready, mvA_ready, T + 1)
                    elif name == "a_norm":
                        dve.wait_ge(rstdA_ready, T + 1)
                        dve.wait_ge(mvA_ready, T + 1)
                        if not is_first(T):
                            dve.wait_ge(x0_stored, 16 * T)
                            dve.wait_ge(rxT_ps, T)
                        v.tensor_scalar(x0[:, :], rA[:, :], mvA[:, 0:1], rstdA[:, 0:1], ALU.subtract, ALU.mult)\
                            .then_inc(x0_ready, 1)
                    elif name == "a_qkf":
                        dve.wait_ge(qk_ps, T + 1)
                        if not is_first(T):
                            dve.wait_ge(parts_ready, T)
                        v.tensor_tensor(qkf[:, :, :], abank[:, :].rearrange("p (c t) -> p c t", c=2 * EC),
                                        qkb[:, :].unsqueeze(2).broadcast_to([P, 2 * EC, P]), ALU.add)\
                            .then_inc(qkf_ready, 1)
                    elif name == "a_vst":
                        dve.wait_ge(v_ps, T + 1)
                        if not is_first(T):
                            dve.wait_ge(v_stored, 16 * T)
                        v.tensor_tensor(vst[:, :, 0:DH], abank[:, 0:E].rearrange("p (h d) -> p h d", h=H),
                                        b_v.rearrange("p (h d) -> p h d", h=H), ALU.add).then_inc(vst_ready, 1)
                    elif name == "d_res":
                        dve.wait_ge(oD_ps, TD + 1)
                        dve.wait_ge(x0b_ready, TD + 1)
                        v.tensor_tensor(rD[:, :], dbank[:, 0:E], x0b[:, :], ALU.add).then_inc(rD_ready, 1)
                        dve.wait_ge(rD_ready, TD + 1)
                        moments(rD[:, :], stD, mvD, stD_ready, mvD_ready, TD + 1)
                    elif name == "d_norm":
                        dve.wait_ge(rstdD_ready, TD + 1)
                        dve.wait_ge(mvD_ready, TD + 1)
                        v.tensor_scalar(rD[:, :], rD[:, :], mvD[:, 0:1], rstdD[:, 0:1], ALU.subtract, ALU.mult)\
                            .then_inc(xh_ready, 1)
                    elif name == "f_lg":
                        if is_first(TF):
                            dve.wait_ge(moe_loaded, 16 * MOE_LOADS)
                        dve.wait_ge(g_ps, TF + 1)
                        v.tensor_tensor(lg[:, :], dbank[:, 0:NE], gb_sb[:, :], ALU.add).then_inc(lg_ready, 1)
                        dve.wait_ge(lg_ready, TF + 1)
                        v.tensor_reduce(ngm[:, :], lg[:, :], AX_X, ALU.max, negate=True).then_inc(ngm_ready, 1)
                    elif name == "f_top":
                        dve.wait_ge(ge_ready, TF + 1)
                        v.reciprocal(gr[:, :], gsum[:, :]).then_inc(top_step, 1)
                        dve.wait_ge(top_step, NTOP * TF + 1)
                        v.tensor_scalar(gates[:, :], ge[:, :], gr[:, 0:1], None, ALU.mult).then_inc(top_step, 1)
                        dve.wait_ge(top_step, NTOP * TF + 2)
                        settled(dve)
                        v.max(top8[:, :], gates[:, :]).then_inc(top_step, 1)
                        dve.wait_ge(top_step, NTOP * TF + 3)
                        settled(dve)
                        v.max_index(ix8[:, :], top8[:, :], gates[:, :]).then_inc(top_step, 1)
                        dve.wait_ge(top_step, NTOP * TF + 4)
                        v.tensor_copy(ixf[:, :], ix8[:, :]).then_inc(top_step, 1)
                        dve.wait_ge(top_step, NTOP * TF + 5)
                        for k, w in enumerate((w1st, w2nd)):
                            v.scalar_tensor_tensor(out=w[:, :], in0=iota8[:, :], scalar=ixf[:, k:k + 1],
                                                   in1=gates[:, :], op0=ALU.is_equal, op1=ALU.mult)\
                                .then_inc(top_step, 1)
                        dve.wait_ge(top_step, NTOP * TF + 7)
                        v.tensor_tensor(wts[:, :], w1st[:, :], w2nd[:, :], ALU.add).then_inc(wts_ready, 1)
                    elif name == "f_acc0":
                        dve.wait_ge(eb_ps, TF + 1)
                        dve.wait_ge(x1_ready, TF + 1)
                        if not is_first(TF):
                            dve.wait_ge(out_stored, 16 * TF)
                        v.tensor_tensor(acc[:, :], dbank[:, 0:E], x1[:, :], ALU.add).then_inc(acc_step, 1)
                    elif name in ("f_e0c", "f_e2c"):
                        k = int(name[3])
                        dve.wait_ge(e_ps, 4 * TF + k + 1)
                        for e in range(2):
                            dve.wait_ge(acc_step, 5 * TF + k + e + 1)
                            v.scalar_tensor_tensor(out=acc[:, :], in0=dbank[:, e * E:(e + 1) * E],
                                                   scalar=wts[:, 2 * k + e:2 * k + e + 1], in1=acc[:, :],
                                                   op0=ALU.mult, op1=ALU.add).then_inc(acc_step, 1)
                    elif name == "f_y":
                        dve.wait_ge(accp_step, 3 * TF + 3)
                        dve.wait_ge(acc_step, 5 * TF + 5)
                        v.tensor_tensor(acc[:, :], acc[:, :], accp[:, :], ALU.add).then_inc(y_ready, 1)
                        dve.wait_ge(y_ready, TF + 1)
                        moments(acc[:, :], stF, mvF, stF_ready, mvF_ready, 2 * TF + 1)
                    elif name == "f_norm2":
                        dve.wait_ge(rstdF_ready, 2 * TF + 1)
                        dve.wait_ge(mvF_ready, 2 * TF + 1)
                        v.tensor_scalar(xh2, acc[:, :], mvF[:, 0:1], rstdF[:, 0:1], ALU.subtract, ALU.mult)\
                            .then_inc(xh2_ready, 1)
                    elif name == "f_z":
                        dve.wait_ge(z_ready, TF + 1)
                        moments(acc[:, :], stF, mvF, stF_ready, mvF_ready, 2 * TF + 2)
                    elif name == "f_norm3":
                        dve.wait_ge(rstdF_ready, 2 * TF + 2)
                        dve.wait_ge(mvF_ready, 2 * TF + 2)
                        v.tensor_scalar(acc[:, :], acc[:, :], mvF[:, 0:1], rstdF[:, 0:1], ALU.subtract, ALU.mult)\
                            .then_inc(ob_ready, 1)

            walk(dve, body)

        @block.tensor
        def _(pe):
            mm, tr = nc.tensor.matmul, nc.tensor.transpose
            pe.wait_ge(fold_loaded, 16 * FOLD_LOADS)
            wqkt = pbuf[:, 0:2, :].rearrange("p a b -> p (a b)").rearrange("p (c d) -> p c d", c=2 * EC)
            woutn = pbuf[:, 2, :].rearrange("p (c d) -> p c d", c=EC)
            for k, (lc, rhs) in enumerate(((0, wqkt[:, EC:2 * EC, :]), (EC, woutn))):
                for d in range(EC):
                    for e in range(EC):
                        last = mm(bank[k][:, d * E:(d + 1) * E], wqkt[:, lc + e, d * P:(d + 1) * P], rhs[:, e, :],
                                  start=e == 0, stop=e == EC - 1)
                last.then_inc(fold_ps, 1)
            pe.wait_ge(folded, 2)
            pe.wait_ge(consts, 9)
            pe.wait_ge(dve_set, 4)

            def wait_context_bank(t):
                pe.wait_ge(ctx_ready, GT * t.st[0] + t.st[1] if t.st else GT * NG)

            def body(t):
                T, TF = t.at, t.ft
                if t.dt:
                    TD = GT * t.dt[0] + t.dt[1]
                for step in t.steps:
                    name = step[0]
                    if name == "mx":
                        sm, um = t.mx
                        c, j, h = step[1:]
                        g = keys_groups(sm)
                        i = (c * GT + j) * HJ + h
                        base = units_before(sm, um)
                        diag = c == g - 1
                        width = (j + 1) * P if diag else GQ
                        if i == 0 and is_first(um):
                            pe.wait_ge(stack_loaded, 16 * 2 * SLOTS * GT * (sm + 1))
                        if not (is_first(base) and i < MXB):
                            pe.wait_ge(mx_used, base + i - MXB + 1)
                        qcol = (um * HJ + h) * (QRING * GQ) + (sm % QRING) * GQ + j * P
                        kcol = (um * HJ + h) * (KRING * GQ) + (((sm // GB) * GB + c) % KRING) * GQ
                        bk = mxbank[i % MXB]
                        last = mm(bk[:, 0:width], qs[0:KR, ds(qcol, P)], ks[0:KR, ds(kcol, width)],
                                  start=True, stop=not diag)
                        if diag:
                            last = mm(bk[:, j * P:(j + 1) * P], idb[:, :], maskb[:, :], start=False, stop=True)
                        last.then_inc(mx_ready, 1)
                    elif name == "nm_T":
                        job = GT * t.mx[0] + t.mx[1]
                        pe.wait_ge(nm_step, NCHAINM * (job + 1))
                        if t.at is not None:
                            pe.wait_ge(vst_ready, T + 1)
                        elif not is_first(job):
                            pe.wait_ge(nmT_ready, job)
                        for j in range(GT):
                            last = tr(nmbank[:, j * P:(j + 1) * P],
                                      nmp[:, j, :, :].rearrange("p h a -> p (h a)"), idb[:, :])
                        last.then_inc(nmT_ps, 1)
                    elif name == "st":
                        sj, hg = t.st
                        kb, h = step[1:]
                        i = kb * HJ + h
                        base = units_before(sj, hg)
                        first_diag = key_tiles(sj) - GT
                        r0 = max(0, kb - first_diag) * P
                        if i == 0 and is_first(base):
                            pe.wait_ge(ones_loaded, 16)
                        if i == 0:
                            pe.wait_ge(nm_loaded, 16 * HJ * (GT * sj + hg + 1))
                        if i >= STB:
                            pe.wait_ge(exp_done, base + i - STB + 1)
                        elif not is_first(base):
                            pe.wait_ge(exp_done, base)
                        kcol = (hg * HJ + h) * (KRING * GQ) + (((sj // GB) * GB + kb // GT) % KRING) * GQ + kb % GT * P
                        qcol = (hg * HJ + h) * (QRING * GQ) + (sj % QRING) * GQ + r0
                        bk = stbank[i % STB]
                        last = mm(bk[:, r0:GQ], ks[0:KR + NPART, ds(kcol, P)], qs[0:KR + NPART, ds(qcol, GQ - r0)],
                                  start=True, stop=kb < first_diag)
                        if kb >= first_diag:
                            last = mm(bk[:, r0:r0 + P], maskb[:, :], idb[:, :], start=False, stop=True)
                        last.then_inc(st_ready, 1)
                    elif name == "pv":
                        sj, hg = t.st
                        kb = step[1]
                        last_kb = key_tiles(sj) - 1
                        jj = kb - (last_kb + 1 - GT)
                        r0 = max(0, jj) * P
                        job = GT * sj + hg
                        pe.wait_ge(exp_done, units_before(sj, hg) + HJ * (kb + 1))
                        if kb % GT == 0:
                            pe.wait_ge(vcur_loaded[kb // GT], 16 * (loads_before(sj, hg, kb // GT) + 1))
                        if kb == 0 and not is_first(job):
                            pe.wait_ge(osb_ready, job)
                        for h in range(HJ):
                            last = mm(obank[32 * h:32 * h + DV, r0:GQ], vcur[:, kb, h, :],
                                      pbuf[:, (kb * HJ + h) % PB, r0:GQ], start=kb == 0, stop=kb == last_kb,
                                      tile_position=(0, 32 * h))
                        last.then_inc(pv_done, 1)
                    elif name == "o_T":
                        job = GT * t.st[0] + t.st[1]
                        pe.wait_ge(osb_ready, job + 1)
                        if t.dt:
                            pe.wait_ge(x1T_ready, TD + 1)
                        elif t.ft is not None:
                            pe.wait_ge(etmp_ready, 2 * (TF + 1))
                        elif not is_first(job):
                            pe.wait_ge(ctx_ready, job)
                        for j in range(GT):
                            last = tr(dbank[:, j * P:(j + 1) * P], osb[:, j * P:(j + 1) * P], idf[:, :])
                        last.then_inc(oT_ps, 1)
                    elif name == "a_xT":
                        pe.wait_ge(xw_loaded, 16 * (T + 1))
                        if t.mx and not is_first(t.mx[1] + GT * t.mx[0]):
                            pe.wait_ge(nmT_ready, GT * t.mx[0] + t.mx[1])
                        elif not is_first(T):
                            pe.wait_ge(vst_ready, T)
                        for c in range(EC):
                            for w in range(2):
                                last = tr(abank[:, (2 * c + w) * P:(2 * c + w + 1) * P], xw[:, w, c * P:(c + 1) * P],
                                          idf[:, :])
                        last.then_inc(xT_ps, 1)
                    elif name == "a_q":
                        pe.wait_ge(xT_ready, T + 1)
                        for co in range(EC):
                            for ci in range(EC):
                                last = mm(abank[:, co * P:(co + 1) * P], m_sb[:, ci, co * P:(co + 1) * P],
                                          xT[:, ci, P:2 * P], start=ci == 0, stop=ci == EC - 1)
                        last.then_inc(qT_ps, 1)
                    elif name == "a_s":
                        pe.wait_ge(qT_ready, T + 1)
                        for c in range(EC):
                            mm(abank[:, 0:2 * P], qT[:, c, :], xT[:, c, :], start=c == 0, stop=False)
                        mm(abank[:, P:2 * P], idb[:, :], maskb[:, :], start=False, stop=True).then_inc(sA_ps, 1)
                    elif name == "a_pT":
                        pe.wait_ge(pA_ready, T + 1)
                        for w in range(2):
                            last = tr(abank[:, w * P:(w + 1) * P], pA[:, w * P:(w + 1) * P], idf[:, :])
                        last.then_inc(pT_ps, 1)
                    elif name == "a_y":
                        pe.wait_ge(pT_ready, T + 1)
                        for c in range(EC):
                            for w in range(2):
                                last = mm(abank[:, c * P:(c + 1) * P], xw[:, w, c * P:(c + 1) * P], pT[:, w, :],
                                          start=w == 0, stop=w == 1)
                        last.then_inc(yT_ps, 1)
                    elif name == "a_o":
                        pe.wait_ge(yT_ready, T + 1)
                        for c in range(EC):
                            last = mm(abank[:, 0:E], yT[:, c, :], wko[:, c, :], start=c == 0, stop=c == EC - 1)
                        last.then_inc(oA_ps, 1)
                    elif name == "a_rT":
                        pe.wait_ge(rp_ready, T + 1)
                        for c in range(2 * EC):
                            src = (rp if c < EC else x0)[:, (c % EC) * P:(c % EC + 1) * P]
                            last = tr(abank[:, c * P:(c + 1) * P], src, idf[:, :])
                        last.then_inc(rxT_ps, 1)
                    elif name == "a_qk":
                        pe.wait_ge(rxT_ready, T + 1)
                        for co in range(2 * EC):
                            for ci in range(EC):
                                last = mm(abank[:, co * P:(co + 1) * P], inw[:, ci, co * P:(co + 1) * P],
                                          rxT[:, ci, :], start=ci == 0, stop=ci == EC - 1)
                        last.then_inc(qk_ps, 1)
                    elif name == "a_v":
                        pe.wait_ge(qkf_ready, T + 1)
                        for ci in range(EC):
                            last = mm(abank[:, 0:E], rxT[:, EC + ci, :], inw[:, ci, 2 * E:3 * E],
                                      start=ci == 0, stop=ci == EC - 1)
                        last.then_inc(v_ps, 1)
                    elif name == "d_cT":
                        pe.wait_ge(cj_ready, TD + 1)
                        if t.ft is not None:
                            pe.wait_ge(lg_ready, TF + 1)
                        else:
                            wait_context_bank(t)
                        for c in range(EC):
                            last = tr(dbank[:, c * P:(c + 1) * P], cj[:, c * P:(c + 1) * P], idf[:, :])
                        last.then_inc(cT_ps, 1)
                    elif name == "d_o":
                        pe.wait_ge(cT_ready, TD + 1)
                        if is_first(TD):
                            pe.wait_ge(moe_loaded, 16 * MOE_LOADS)
                        for c in range(EC):
                            last = mm(dbank[:, 0:E], cT[:, c, :], wo[:, c, :], start=c == 0, stop=c == EC - 1)
                        last.then_inc(oD_ps, 1)
                    elif name == "d_x1T":
                        pe.wait_ge(x1_ready, TD + 1)
                        if t.ft is not None:
                            pe.wait_ge(etmp_ready, 2 * (TF + 1))
                        for c in range(EC):
                            last = tr(dbank[:, c * P:(c + 1) * P], x1[:, c * P:(c + 1) * P], idf[:, :])
                        last.then_inc(x1T_ps, 1)
                    elif name == "f_g":
                        pe.wait_ge(x1T_ready, TF + 1)
                        wait_context_bank(t)
                        for c in range(EC):
                            last = mm(dbank[:, 0:NE], x1T[:, c, :], gw[:, c, :], start=c == 0, stop=c == EC - 1)
                        last.then_inc(g_ps, 1)
                    elif name == "f_wT":
                        pe.wait_ge(wts_ready, TF + 1)
                        if t.dt:
                            pe.wait_ge(rD_ready, TD + 1)
                        tr(dbank[0:NE, 0:P], wts[:, :], idf[:, :]).then_inc(wT_ps, 1)
                    elif name == "f_b":
                        pe.wait_ge(wT_ready, TF + 1)
                        mm(dbank[:, 0:E], wT[:, :], eb[:, :], start=True, stop=True).then_inc(eb_ps, 1)
                    elif name in ("f_e0", "f_e1", "f_e2", "f_e3"):
                        k = int(name[3])
                        if k == 0:
                            pe.wait_ge(acc_step, 5 * TF + 1)
                        elif k == 2:
                            pe.wait_ge(etmp_ready, 2 * TF + 1)
                        else:
                            pe.wait_ge(acc_step, 5 * TF + k + 2)
                        for c in range(EC):
                            last = mm(dbank[:, :], x1T[:, c, :], ew[:, c, k * 2 * E:(k + 1) * 2 * E],
                                      start=c == 0, stop=c == EC - 1)
                        last.then_inc(e_ps, 1)

            walk(pe, body)


def kernel(L0_attn_x, L0_attn_w_qkv, L0_attn_w_out, L0_attn_b_out, L0_ffn_in_proj_w, L0_ffn_in_proj_b,
           L0_ffn_out_proj_w, L0_ffn_out_proj_b, L0_ffn_gate_w, L0_ffn_gate_b, L0_ffn_expert_w, L0_ffn_expert_b,
           L0_ffn_ln1_w, L0_ffn_ln1_b, L0_ffn_ln2_w, L0_ffn_ln2_b):
    import concourse.bacc as bacc
    from concourse.bass_utils import run_bass_kernel_spmd as run

    windows = np.zeros((NT + 1, 2, P, E), np.float32)
    tiles = np.asarray(L0_attn_x).reshape(B, TB, P, E)
    windows[:NT, 1] = tiles.reshape(NT, P, E)
    windows[:NT, 0].reshape(B, TB, P, E)[:, 1:] = tiles[:, :-1]
    inv_freq = (1.0 / np.float32(10000.0) ** (np.arange(0, DH, 2, dtype=np.float32) / np.float32(DH)))
    freqs = np.arange(N, dtype=np.float32)[:, None] * inv_freq.astype(np.float32)[None, :]
    cs = np.zeros((N, 2, DH // 2, 2), np.float32)
    cs[:, 0, :, 0] = cs[:, 0, :, 1] = np.cos(freqs)
    cs[:, 1, :, 1] = np.sin(freqs)
    cs[:, 1, :, 0] = -np.sin(freqs)
    rows = np.empty((P, 7, E), np.float32)
    for i, vec in enumerate((L0_attn_b_out, np.asarray(L0_ffn_in_proj_b)[2 * E:], L0_ffn_out_proj_b, L0_ffn_ln1_w,
                             L0_ffn_ln1_b, L0_ffn_ln2_w, L0_ffn_ln2_b)):
        rows[:, i, :] = np.asarray(vec)
    arrays = {
        "windows": windows.reshape((NT + 1) * 2 * P, E),
        "cs": np.concatenate([cs.reshape(N, 2 * DH)] * B + [np.zeros((P, 2 * DH), np.float32)]),
        "w_qk_t": np.asarray(L0_attn_w_qkv)[:, :2 * E].T,
        "w_out": np.asarray(L0_attn_w_out),
        "in_t": np.asarray(L0_ffn_in_proj_w).T,
        "in_b": np.asarray(L0_ffn_in_proj_b)[:2 * E].reshape(2 * EC, P).T,
        "wo_t": np.asarray(L0_ffn_out_proj_w).T,
        "gate_t": np.asarray(L0_ffn_gate_w).T,
        "exp_t": np.asarray(L0_ffn_expert_w).transpose(2, 0, 1).reshape(E, NE * E),
        "exp_b": np.asarray(L0_ffn_expert_b),
        "rows": rows,
        "gate_b": np.broadcast_to(np.asarray(L0_ffn_gate_b)[None, :], (P, NE)),
    }
    arrays = {n: np.ascontiguousarray(a) for n, a in arrays.items()}
    nc = bacc.Bacc("TRN2", target_bir_lowering=False, num_devices=1)
    args = [nc.dram_tensor(n, a.shape, mybir.dt.from_np(a.dtype), kind="ExternalInput").ap()
            for n, a in arrays.items()]
    args.append(nc.dram_tensor("out", (NT * P, E), F32, kind="ExternalOutput").ap())
    build(nc, *args)
    r = run(nc, [arrays], core_ids=[0])
    return r.results[0]["out"].reshape(B, N, E)
```

```python
from contextlib import ExitStack

import numpy as np
import concourse.bass as bass
from concourse import mybir

F32 = mybir.dt.float32
BF16 = mybir.dt.bfloat16
U32 = mybir.dt.uint32
ALU = mybir.AluOpType
ACT = mybir.ActivationFunctionType
AX_X = mybir.AxisListType.X

P = 128
E = 256
EC = E // P
B, N = 2, 2048
H, DH = 16, 16
DV = DH + 1
TB = N // P
NT = B * TB
GT = 4
GQ = GT * P
GB = TB // GT
NG = B * GB
HJ = 4
NE = 8
SLOTS = 6
KR = SLOTS * DH
NPART = 3
Q_PARTS = (0, 0, 0, 1, 1, 2)
K_PARTS = (0, 1, 2, 0, 1, 0)
KRING = GB + 1
QRING = 2
MXB, STB = 3, 2
PB = 8
NEG = -1.0e30
EPS = 1e-5
NCHAINM = 5
NTOP = 7


def ds(start, size):
    return slice(start, start + size) if isinstance(start, int) else bass.ds(start, size)


def is_first(count):
    return isinstance(count, int) and count == 0


def keys_groups(s):
    return s % GB + 1


def units(s):
    return 16 * keys_groups(s)


def units_before(s, hg):
    return sum(HJ * units(x) for x in range(s)) + hg * units(s)


def key_tiles(s):
    return GT * keys_groups(s)


def key_tiles_before(s, hg):
    return sum(HJ * key_tiles(x) for x in range(s)) + hg * key_tiles(s)


def loads_before(s, hg, c):
    return sum(4 for x in range(s) if x % GB >= c) + hg


AR_CHAIN = """a_xT:12 r_rope:8 a_xTc:10 a_xb:2 a_q:20 a_qc:12 r_rT:10 r_rTc:10 a_s:16 a_max:10 a_exp:10
r_load_cs:1 r_qk:22 r_qkf:12 r_split:3 a_pT:10 a_pTc:10 r_v:12 r_vst:8 r_vstore:1 a_y:15 a_yc:5 a_load:1 a_o:16
a_res:22 a_rstd:14 r_pst:0 a_norm:8 a_st0:5"""
DF_CHAIN = """d_load0:3 d_cp:1 f_g:17 f_lg:8 d_xb:10 d_cT:12 d_cTc:12 f_exp:14 d_o:25 f_top:15 d_res:15
d_load:0 d_rstd:5 f_wT:12 f_wTc:12 f_b:12 d_norm:10 f_acc0:8 d_aff:7 f_e0:16 f_e0c:16 f_e1:27 f_e1c:14 f_e1a:21
f_e2:27 f_e2c:16 f_e3:27 f_e3c:16 d_x1T:12 d_x1Tc:12 f_e3a:20 f_load:4"""
G_CHAIN = """g_y:74 g_rstd2:4 g_norm2:8 g_xb:2 g_aff2:14 g_z:10 g_rstd3:17 g_norm3:10 g_store:0"""
SPANS = (
    ((-0.082, 0.847), (0.840, 0.912), (0.040, 1.015), (-0.080, 0.930), (-0.039, 0.970), (-0.002, 0.400)),
    ((-0.082, 0.847), (0.840, 0.912), (0.040, 1.015), (-0.080, 0.899), (-0.039, 0.970), (-0.002, 0.400)),
    ((-0.082, 0.795), (0.830, 0.912), (0.040, 1.015), (-0.080, 0.899), (-0.048, 0.922), (-0.002, 0.400)),
    ((-0.082, 0.847), (0.840, 0.912), (0.035, 1.015), (-0.103, 0.899), (-0.039, 0.970), (-0.002, 0.426)),
    ((-0.067, 0.847), (0.840, 0.904), (0.040, 1.015), (-0.116, 0.904), (-0.065, 0.970), (-0.038, 0.400)),
)


def chain(text, prefixes):
    steps = [x.split(":") for x in text.split() if x[0] in prefixes]
    return [((name,), int(share)) for name, share in steps]


def spread(lists):
    at = []
    for k, (steps, (start, end)) in enumerate(lists):
        total, done = sum(share for _, share in steps), 0
        for i, (x, share) in enumerate(steps):
            at.append((start + (end - start) * done / total, k, i, x))
            done += share
    return [x for _, _, _, x in sorted(at)]


def order(mx_s, st_s, has_a, has_r, has_stack, has_d, has_f, has_g, hold_stack):
    lists = []
    mx_span, nm_span, st_span, ar_span, df_span, g_span = \
        SPANS[keys_groups(mx_s) if mx_s is not None else keys_groups(st_s) if st_s is not None else 0]
    if mx_s is not None:
        g = keys_groups(mx_s)
        lists.append(([(("mx", c, j, h), 1) for c in range(g) for j in range(GT) for h in range(HJ)], mx_span))
        lists.append(([(("nm_d",), 1), (("nm_T",), 0)], nm_span))
    if st_s is not None:
        g, st = keys_groups(st_s), []
        for kb in range(GT * g):
            st += [("st", kb, h) for h in range(HJ)]
            if kb:
                st.append(("pv", kb - 1))
                if kb % GT == 0:
                    st.append(("vload", kb // GT - 1))
        st += [("pv", GT * g - 1), ("vload", g - 1)]
        lists.append(([(x, 1) for x in st], st_span))
    ar = chain(AR_CHAIN, "a" * has_a + "r" * has_r)
    if ar:
        lists.append((ar, ar_span))
    df = chain(DF_CHAIN, "d" * has_d + "f" * has_f)
    if df:
        lists.append((df, df_span))
    if has_g:
        lists.append((chain(G_CHAIN, "g"), g_span))
    steps = [("vload_new",)] + spread(lists)
    if mx_s is not None and has_r:
        assert steps.index(("a_res",) if has_a else ("r_vst",)) < steps.index(("nm_T",))
    if has_f and has_g:
        assert steps.index(("g_aff2",)) < steps.index(("f_acc0",)) and steps.index(("g_store",)) < steps.index(("f_e1c",))
    if has_stack:
        steps.insert(len(steps) if hold_stack else len(steps) // 8, ("a_stack",))
    if st_s is not None:
        steps += [("o_evac",), ("o_T",), ("o_ctx",)]
    return steps


def within(x, limit):
    return 0 <= x < limit


class Turn:

    def __init__(self, s, u0, u):
        n0, first = GT * s + u0, u0 == 0
        self.s, self.u = s, u
        self.mx = (s, u) if within(n0, NT) else None
        self.st = ((s - 1, 3) if first else (s, u - 1)) if within(n0 - 1, NT) else None
        self.at = GT * s + 6 + u if within(n0 + 6, NT) else None
        self.rt = GT * s + 5 + u if within(n0 + 5, NT) else None
        self.stack = (s + 1, u) if within(n0 + 4, NT) else None
        self.dt = ((s - 2, 3) if first else (s - 1, u - 1)) if within(n0 - 5, NT) else None
        self.ft = u + (GT * s - 6) if within(n0 - 6, NT) else None
        self.gt = u + (GT * s - 7) if within(n0 - 7, NT) else None
        self.steps = order(self.mx and s, self.st and self.st[0], self.at is not None, self.rt is not None, self.stack is not None,
                           self.dt is not None, self.ft is not None, self.gt is not None, first and s >= 1)

    @staticmethod
    def kind(s, u):
        n = GT * s + u
        return (u == 0, min(max(n, -1), 2), [within(n + k, NT) for k in (6, 5, 4, 0, -1, -5, -6, -7)],
                [n + k == 0 for k in (6, 5, -5, -6, -7)], n - 5 == NT - 1)


def walk(eng, body):
    for s in range(-2, NG + 2):
        u = 0
        while u < GT:
            end = u + 1
            while end < GT and Turn.kind(s, end) == Turn.kind(s, u):
                end += 1
            if -6 <= GT * s + u < NT + 7:
                if end == u + 1:
                    body(Turn(s, u, u))
                else:
                    with eng.Fori(u, end) as reg:
                        body(Turn(s, u, reg))
            u = end


def build(nc, windows, cs, w_qk_t, w_out, in_t, in_b, wo_t, gate_t, exp_t, exp_b, rows, gate_b, out):
    x0_dram = nc.dram_tensor("x0_scratch", (NT * P, E), F32, kind="Internal").ap()
    v_dram = nc.dram_tensor("v_scratch", (NT * P, H * DV), F32, kind="Internal").ap()
    parts_dram = nc.dram_tensor("parts_scratch", (NT * NPART * 2 * E, P), BF16, kind="Internal").ap()

    with ExitStack() as ctx:
        def sb(name, shape, dt=F32):
            return ctx.enter_context(nc.sbuf_tensor(name, shape, dt))

        def sem(name):
            return ctx.enter_context(nc.semaphore(name))

        idf = sb("idf", [P, P])
        idb = sb("idb", [P, P], BF16)
        maskb = sb("maskb", [P, P], BF16)
        iota8 = sb("iota8", [P, NE])
        mhalf = sb("mhalf", [P, 1])
        m_sb = sb("m_sb", [P, EC, E])
        wko = sb("wko", [P, EC, E])
        inw = sb("inw", [P, EC, 3 * E])
        wo = sb("wo", [P, EC, E])
        gw = sb("gw", [P, EC, NE])
        ew = sb("ew", [P, EC, NE * E])
        eb = sb("eb", [NE, E])
        qkb = sb("qkb", [P, 2 * EC])
        rowv = sb("rowv", [P, 7, E])
        gb_sb = sb("gb_sb", [P, NE])
        b_out, b_v, b_op, g1, b1, g2, b2 = (rowv[:, i, :] for i in range(7))

        qs = sb("qs", [P, H * QRING * GQ], BF16)
        ks = sb("ks", [P, H * KRING * GQ], BF16)
        qs3 = qs[:, :].rearrange("p (h c) -> p h c", h=H)
        ks3 = ks[:, :].rearrange("p (h c) -> p h c", h=H)
        vcur = sb("vcur", [P, TB, HJ, DV])
        pbuf = sb("pbuf", [P, PB, GQ])
        mxs = sb("mxs", [P, GT * HJ, GB])
        nm = sb("nm", [P, GT * HJ])
        nmd = sb("nmd", [P, GT * HJ])
        nmp = sb("nmp", [P, GT, HJ, NPART], BF16)
        nmT = sb("nmT", [NPART * HJ, GQ], BF16)
        osb = sb("osb", [P, GQ])
        oden = sb("oden", [P, GT, HJ])
        ctxn = sb("ctxn", [P, 2 * GT, E])

        xw = sb("xw", [P, 2, E])
        cst = sb("cst", [P, 2, DH])
        xb = sb("xb", [P, E])
        xT = sb("xT", [P, EC, 2 * P])
        qT = sb("qT", [P, EC, P])
        nmA = sb("nmA", [P, 1])
        sumA = sb("sumA", [P, 1])
        rsA = sb("rsA", [P, 1])
        pA = sb("pA", [P, 2 * P])
        pT = pA[:, :].rearrange("p (w t) -> p w t", w=2)
        yT = qT
        rA = xb
        stA = sb("stA", [P, 6])
        mvA = sb("mvA", [P, 2])
        veA = sb("veA", [P, 1])
        rstdA = sb("rstdA", [P, 1])
        x0 = sb("x0", [P, E])
        rp = pA

        rxT = sb("rxT", [P, 2 * EC, P])
        qkf = sb("qkf", [P, 2 * EC, P])
        rps = qkf[:, 0:2, :].rearrange("p c t -> p (c t)")
        parts = sb("parts", [P, NPART, 2 * EC, P], BF16)
        vst = sb("vst", [P, H, DV])

        x0b = sb("x0b", [P, E])
        cj = sb("cj", [P, E])
        cT = sb("cT", [P, EC, P])
        rD = sb("rD", [P, E])
        stD = sb("stD", [P, 6])
        mvD = sb("mvD", [P, 2])
        veD = sb("veD", [P, 1])
        rstdD = sb("rstdD", [P, 1])
        x1 = sb("x1", [P, E])
        x1T = sb("x1T", [P, EC, P])

        lg = sb("lg", [P, NE])
        ngm = sb("ngm", [P, 1])
        ge = sb("ge", [P, NE])
        gsum = sb("gsum", [P, 1])
        gr = sb("gr", [P, 1])
        gates = sb("gates", [P, NE])
        top8 = sb("top8", [P, 8])
        ix8 = sb("ix8", [P, 8], U32)
        ixf = sb("ixf", [P, 8])
        w1st = sb("w1st", [P, NE])
        w2nd = sb("w2nd", [P, NE])
        wts = sb("wts", [P, NE])
        wT = sb("wT", [NE, P])
        acc = sb("acc", [P, E])
        etmp = sb("etmp", [P, 2, E])
        esum, x0f = etmp[:, 0, :], etmp[:, 1, :]
        obuf = esum
        accp = cj
        stF = sb("stF", [P, 6])
        mvF = sb("mvF", [P, 2])
        veF = sb("veF", [P, 1])
        rstdF = sb("rstdF", [P, 1])

        bank = [ctx.enter_context(nc.psum_tensor(f"bank{i}", [P, 512], F32)) for i in range(8)]
        mxbank, stbank, obank, abank, dbank = bank[0:MXB], bank[MXB:MXB + STB], bank[5], bank[6], bank[7]


        def rbank(t):
            return abank if t.mx else mxbank[0]

        def expert_bank(t, k):
            return dbank if t.mx else mxbank[k % 2]

        nmbank = abank[0:NPART * HJ, 0:GQ // 2].bitcast(BF16)

        fold_loaded = sem("fold_loaded")
        proj_loaded = sem("proj_loaded")
        moe_loaded = sem("moe_loaded")
        ones_loaded = sem("ones_loaded")
        consts = sem("consts")
        fold_ps = sem("fold_ps")
        folded = sem("folded")
        dve_set = sem("dve_set")
        mx_ready = sem("mx_ready")
        mx_used = sem("mx_used")
        nm_step = sem("nm_step")
        nmT_ps = sem("nmT_ps")
        nmT_ready = sem("nmT_ready")
        nm_loaded = sem("nm_loaded")
        st_ready = sem("st_ready")
        exp_done = sem("exp_done")
        pv_done = sem("pv_done")
        vcur_loaded = [sem(f"vcur_loaded{c}") for c in range(GB)]
        osb_ready = sem("osb_ready")
        oT_ps = sem("oT_ps")
        oden_ready = sem("oden_ready")
        ctx_ready = sem("ctx_ready")
        xw_loaded = sem("xw_loaded")
        cs_loaded = sem("cs_loaded")
        xT_ps = sem("xT_ps")
        xT_ready = sem("xT_ready")
        xb_ready = sem("xb_ready")
        qT_ps = sem("qT_ps")
        qT_ready = sem("qT_ready")
        sA_ps = sem("sA_ps")
        nmA_ready = sem("nmA_ready")
        pA_ready = sem("pA_ready")
        pT_ps = sem("pT_ps")
        pT_ready = sem("pT_ready")
        yT_ps = sem("yT_ps")
        yT_ready = sem("yT_ready")
        oA_ps = sem("oA_ps")
        rsA_ready = sem("rsA_ready")
        rA_ready = sem("rA_ready")
        stA_ready = sem("stA_ready")
        mvA_ready = sem("mvA_ready")
        veA_ready = sem("veA_ready")
        rstdA_ready = sem("rstdA_ready")
        x0_ready = sem("x0_ready")
        x0_stored = sem("x0_stored")
        rope_step = sem("rope_step")
        rp_ready = sem("rp_ready")
        rxT_ps = sem("rxT_ps")
        rxT_ready = sem("rxT_ready")
        qk_ps = sem("qk_ps")
        qkf_ready = sem("qkf_ready")
        v_ps = sem("v_ps")
        vst_ready = sem("vst_ready")
        v_stored = sem("v_stored")
        split_step = sem("split_step")
        parts_ready = sem("parts_ready")
        parts_stored = sem("parts_stored")
        stack_loaded = sem("stack_loaded")
        x0b_loaded = sem("x0b_loaded")
        cj_ready = sem("cj_ready")
        cT_ps = sem("cT_ps")
        cT_ready = sem("cT_ready")
        x0b_ready = sem("x0b_ready")
        oD_ps = sem("oD_ps")
        rD_ready = sem("rD_ready")
        stD_ready = sem("stD_ready")
        mvD_ready = sem("mvD_ready")
        veD_ready = sem("veD_ready")
        rstdD_ready = sem("rstdD_ready")
        xh_ready = sem("xh_ready")
        x1_ready = sem("x1_ready")
        x1T_ps = sem("x1T_ps")
        x1T_ready = sem("x1T_ready")
        g_ps = sem("g_ps")
        lg_ready = sem("lg_ready")
        ngm_ready = sem("ngm_ready")
        ge_ready = sem("ge_ready")
        top_step = sem("top_step")
        wts_ready = sem("wts_ready")
        wT_ps = sem("wT_ps")
        wT_ready = sem("wT_ready")
        eb_ps = sem("eb_ps")
        acc_step = sem("acc_step")
        e_ps = sem("e_ps")
        etmp_ready = sem("etmp_ready")
        accp_step = sem("accp_step")
        y_ready = sem("y_ready")
        stF_ready = sem("stF_ready")
        mvF_ready = sem("mvF_ready")
        veF_ready = sem("veF_ready")
        rstdF_ready = sem("rstdF_ready")
        xh2_ready = sem("xh2_ready")
        x0f_loaded = sem("x0f_loaded")
        x0fb_ready = sem("x0fb_ready")
        z_ready = sem("z_ready")
        ob_ready = sem("ob_ready")
        out_stored = sem("out_stored")

        waited = {e.engine: sem(f"waited_{i}") for i, e in enumerate((nc.sync, nc.gpsimd, nc.vector))}
        FOLD_LOADS, PROJ_LOADS, MOE_LOADS = 2, 3, 6

        def settled(eng):
            eng.sem_inc(waited[eng.engine], 1)

        block = ctx.enter_context(nc.Block())

        @block.sync
        def _(sp):
            wqkt = pbuf[:, 0:2, :].rearrange("p a b -> p (a b)").rearrange("p (c d) -> p c d", c=2 * EC)
            woutn = pbuf[:, 2, :].rearrange("p (c d) -> p c d", c=EC)

            def load_windows(T):
                sp.dma_start(xw[:, :, :], windows[ds(T * (2 * P), 2 * P), :].rearrange("(w p) d -> p w d", p=P))\
                    .then_inc(xw_loaded, 16)

            def load_angles(T):
                sp.dma_start(cst[:, :, :].rearrange("p k i -> p (k i)"), cs[ds(T * P, P), :]).then_inc(cs_loaded, 16)

            for dst, src in ((wqkt, w_qk_t.rearrange("(c p) d -> p c d", p=P)),
                             (woutn, w_out.rearrange("(c p) d -> p c d", p=P))):
                sp.dma_start(dst, src).then_inc(fold_loaded, 16)
            load_windows(0)
            for dst, src in ((inw[:, :, :], in_t.rearrange("(c p) d -> p c d", p=P)), (qkb[:, :], in_b),
                             (rowv[:, :, :], rows)):
                sp.dma_start(dst, src).then_inc(proj_loaded, 16)
            load_angles(0)
            sp.wait_ge(dve_set, 2)
            sp.dma_start(ks3[KR:KR + NPART, 1:H, :],
                         ks3[KR:KR + NPART, 0:1, :].broadcast_to([NPART, H - 1, KRING * GQ])).then_inc(ones_loaded, 16)
            for dst, src in (
                (wo[:, :, :], wo_t.rearrange("(c p) d -> p c d", p=P)),
                (gw[:, :, :], gate_t.rearrange("(c p) d -> p c d", p=P)),
                (gb_sb[:, :], gate_b),
                (eb[:, :], exp_b),
                (ew[:, 0, :], exp_t[0:P, :]),
                (ew[:, 1, :], exp_t[P:2 * P, :]),
            ):
                sp.dma_start(dst, src).then_inc(moe_loaded, 16)

            def body(t):
                T, TR, TF, TG = t.at, t.rt, t.ft, t.gt
                if t.dt:
                    TD = GT * t.dt[0] + t.dt[1]
                for step in t.steps:
                    name = step[0]
                    if name == "a_load":
                        sp.wait_ge(xb_ready, T + 1)
                        sp.wait_ge(yT_ps, T + 1)
                        load_windows(T + 1)
                    elif name == "r_load_cs":
                        sp.wait_ge(rp_ready, TR + 1)
                        load_angles(TR + 1)
                    elif name == "a_st0":
                        sp.wait_ge(x0_ready, T + 1)
                        sp.dma_start(x0_dram[ds(T * P, P), :], x0[:, :]).then_inc(x0_stored, 16)
                    elif name == "r_vstore":
                        sp.wait_ge(vst_ready, TR + 1)
                        sp.dma_start(v_dram[ds(TR * P, P), :], vst[:, :, :].rearrange("p h d -> p (h d)"))\
                            .then_inc(v_stored, 16)
                    elif name == "r_pst":
                        sp.wait_ge(parts_ready, TR + 1)
                        sp.dma_start(parts_dram[ds(TR * (NPART * 2 * E), NPART * 2 * E), :]
                                     .rearrange("(x p) t -> p x t", p=P),
                                     parts[:, :, :, :].rearrange("p a c t -> p (a c) t")).then_inc(parts_stored, 16)
                    elif name == "a_stack":
                        sa, ua = t.stack
                        TS = GT * sa + ua
                        sp.wait_ge(parts_stored, 16 * (TS + 1))
                        if is_first(ua) and sa >= 2:
                            sp.wait_ge(pv_done, key_tiles_before(sa - 1, 0))
                        for q, (dst, ring, a_of) in enumerate(((qs3, QRING, Q_PARTS), (ks3, KRING, K_PARTS))):
                            col = (sa % ring) * GQ + ua * P
                            for slot, a in enumerate(a_of):
                                r0 = TS * (NPART * 2 * E) + (a * 2 + q) * E
                                sp.dma_start(dst[slot * DH:(slot + 1) * DH, :, ds(col, P)],
                                             parts_dram[ds(r0, E), :].rearrange("(h d) t -> d h t", d=DH))\
                                    .then_inc(stack_loaded, 16)
                    elif name in ("vload_new", "vload"):
                        if not t.mx:
                            continue
                        sm, um = t.mx
                        held = keys_groups(t.st[0]) if t.st else 0
                        if name == "vload_new":
                            if is_first(um):
                                sp.wait_ge(v_stored, 16 * GT * (sm + 1))
                            if t.st and held < keys_groups(sm):
                                sp.wait_ge(pv_done, key_tiles_before(*t.st))
                            chunks = range(held, keys_groups(sm))
                        else:
                            c = step[1]
                            chunks = [c] if c < keys_groups(sm) else []
                            if chunks:
                                sp.wait_ge(pv_done, key_tiles_before(*t.st) + GT * (c + 1))
                        for c in chunks:
                            r0 = ((sm // GB) * TB + c * GT) * P
                            sp.dma_start(vcur[:, GT * c:GT * (c + 1), :, :].rearrange("p k h d -> p k (h d)"),
                                         v_dram[r0:r0 + GT * P, ds(um * (HJ * DV), HJ * DV)]
                                         .rearrange("(k p) x -> p k x", p=P)).then_inc(vcur_loaded[c], 16)
                    elif name == "nm_T":
                        sm, um = t.mx
                        sp.wait_ge(nmT_ready, GT * sm + um + 1)
                        for h in range(HJ):
                            sp.dma_start(qs[KR:KR + NPART, ds((um * HJ + h) * (QRING * GQ) + (sm % QRING) * GQ, GQ)],
                                         nmT[h * NPART:(h + 1) * NPART, :]).then_inc(nm_loaded, 16)
                    elif name == "d_load0":
                        if is_first(TD):
                            sp.wait_ge(x0_stored, 16)
                            sp.dma_start(x0b[:, :], x0_dram[0:P, :]).then_inc(x0b_loaded, 16)
                    elif name == "d_load":
                        if not (isinstance(TD, int) and TD == NT - 1):
                            sp.wait_ge(x0_stored, 16 * (TD + 2))
                            settled(sp)
                            sp.wait_ge(rD_ready, TD + 1)
                            sp.dma_start(x0b[:, :], x0_dram[ds((TD + 1) * P, P), :]).then_inc(x0b_loaded, 16)
                    elif name == "f_load":
                        sp.wait_ge(accp_step, 3 * TF + 3)
                        sp.dma_start(x0f, x0_dram[ds(TF * P, P), :]).then_inc(x0f_loaded, 16)
                    elif name == "g_store":
                        sp.wait_ge(ob_ready, TG + 1)
                        sp.dma_start(out[ds(TG * P, P), :], obuf).then_inc(out_stored, 16)

            walk(sp, body)
            sp.wait_ge(xw_loaded, 16 * (NT + 1))
            sp.wait_ge(cs_loaded, 16 * (NT + 1))
            sp.wait_ge(x0_stored, 16 * NT)
            sp.wait_ge(v_stored, 16 * NT)
            sp.wait_ge(parts_stored, 16 * NT)
            sp.wait_ge(out_stored, 16 * NT)

        @block.gpsimd
        def _(pool):
            pool.memset(idf[:, :], 0.0).then_inc(consts, 1)
            pool.memset(idb[:, :], 0.0).then_inc(consts, 1)
            pool.memset(maskb[:, :], 0.0).then_inc(consts, 1)
            pool.memset(mhalf[:, :], -0.5).then_inc(consts, 1)
            pool.memset(vst[:, :, :], 1.0).then_inc(consts, 1)
            pool.iota(iota8[:, :], pattern=[[1, NE]], base=0, channel_multiplier=0,
                      allow_small_or_imprecise_dtypes=True).then_inc(consts, 1)
            pool.wait_ge(consts, 6)
            for m in (idf, idb):
                pool.affine_select(out=m[:, :], in_=m[:, :], compare_op=ALU.not_equal, fill=1.0, base=0,
                                   pattern=[[-1, P]], channel_multiplier=1).then_inc(consts, 1)
            pool.affine_select(out=maskb[:, :], in_=maskb[:, :], compare_op=ALU.is_ge, fill=NEG, base=0,
                               pattern=[[-1, P]], channel_multiplier=1).then_inc(consts, 1)
            pool.wait_ge(proj_loaded, 16 * PROJ_LOADS)

            def body(t):
                T, TR, TF, TG = t.at, t.rt, t.ft, t.gt
                if t.dt:
                    sd, ud = t.dt
                    TD = GT * sd + ud
                for step in t.steps:
                    name = step[0]
                    if name == "a_xb":
                        pool.wait_ge(xw_loaded, 16 * (T + 1))
                        if not is_first(T):
                            pool.wait_ge(x0_ready, T)
                        pool.tensor_tensor(xb[:, :], xw[:, 1, :], b_out, ALU.add).then_inc(xb_ready, 1)
                    elif name == "a_rstd":
                        pool.wait_ge(mvA_ready, T + 1)
                        settled(pool)
                        pool.tensor_scalar(veA[:, :], mvA[:, 1:2], EPS, None, ALU.add).then_inc(veA_ready, 1)
                        pool.wait_ge(veA_ready, T + 1)
                        pool.tensor_tensor(rstdA[:, :], veA[:, :], mhalf[:, :], ALU.pow).then_inc(rstdA_ready, 1)
                    elif name == "r_rope":
                        pool.wait_ge(x0_ready, TR + 1)
                        pool.wait_ge(cs_loaded, 16 * (TR + 1))
                        if not is_first(TR):
                            pool.wait_ge(rxT_ps, TR)
                        xv = x0[:, :].rearrange("p (h i e) -> p h i e", h=H, e=2)
                        cosv = cst[:, 0, :].unsqueeze(1).broadcast_to([P, H, DH])
                        sv = cst[:, 1, :].rearrange("p (i e) -> p i e", e=2)
                        rsv = rps.rearrange("p (h i e) -> p h i e", h=H, e=2)
                        pool.tensor_tensor(rp[:, :].rearrange("p (h i) -> p h i", h=H),
                                           x0[:, :].rearrange("p (h i) -> p h i", h=H), cosv, ALU.mult)\
                            .then_inc(rope_step, 1)
                        for e in range(2):
                            pool.tensor_tensor(rsv[:, :, :, e], xv[:, :, :, 1 - e],
                                               sv[:, :, e].unsqueeze(1).broadcast_to([P, H, DH // 2]), ALU.mult)\
                                .then_inc(rope_step, 1)
                        pool.wait_ge(rope_step, 3 * (TR + 1))
                        pool.tensor_tensor(rp[:, :], rp[:, :], rps, ALU.add).then_inc(rp_ready, 1)
                    elif name == "r_split":
                        pool.wait_ge(qkf_ready, TR + 1)
                        if not is_first(TR):
                            pool.wait_ge(parts_stored, 16 * TR)
                        settled(pool)
                        pool.tensor_copy(parts[:, 0, :, :], qkf[:, :, :]).then_inc(split_step, 1)
                        pool.wait_ge(split_step, 3 * TR + 1)
                        pool.tensor_tensor(qkf[:, :, :], qkf[:, :, :], parts[:, 0, :, :], ALU.subtract)\
                            .then_inc(split_step, 1)
                        pool.wait_ge(split_step, 3 * TR + 2)
                        settled(pool)
                        pool.tensor_copy(parts[:, 1, :, :], qkf[:, :, :]).then_inc(split_step, 1)
                        pool.wait_ge(split_step, 3 * TR + 3)
                        pool.tensor_tensor(parts[:, 2, :, :], qkf[:, :, :], parts[:, 1, :, :], ALU.subtract)\
                            .then_inc(parts_ready, 1)
                    elif name == "d_cp":
                        sd, ud = t.dt
                        pool.wait_ge(ctx_ready, GT * (sd + 1))
                        if is_first(TD - 1):
                            pool.wait_ge(cT_ps, TD)
                        elif not is_first(TD):
                            pool.wait_ge(accp_step, 3 * TD - 3)
                        settled(pool)
                        pool.tensor_copy(cj[:, :], ctxn[:, ds((sd % 2) * GT + ud, 1), :]
                                         .rearrange("p a b -> p (a b)")).then_inc(cj_ready, 1)
                    elif name == "d_xb":
                        pool.wait_ge(x0b_loaded, 16 * (TD + 1))
                        pool.tensor_tensor(x0b[:, :], x0b[:, :], b_op, ALU.add).then_inc(x0b_ready, 1)
                    elif name == "d_rstd":
                        pool.wait_ge(mvD_ready, TD + 1)
                        settled(pool)
                        pool.tensor_scalar(veD[:, :], mvD[:, 1:2], EPS, None, ALU.add).then_inc(veD_ready, 1)
                        pool.wait_ge(veD_ready, TD + 1)
                        pool.tensor_tensor(rstdD[:, :], veD[:, :], mhalf[:, :], ALU.pow).then_inc(rstdD_ready, 1)
                    elif name in ("g_rstd2", "g_rstd3"):
                        k = int(name[-1]) - 1
                        pool.wait_ge(mvF_ready, 2 * TG + k)
                        settled(pool)
                        pool.tensor_scalar(veF[:, :], mvF[:, 1:2], EPS, None, ALU.add).then_inc(veF_ready, 1)
                        pool.wait_ge(veF_ready, 2 * TG + k)
                        pool.tensor_tensor(rstdF[:, :], veF[:, :], mhalf[:, :], ALU.pow).then_inc(rstdF_ready, 1)
                    elif name == "f_e1a":
                        pool.wait_ge(etmp_ready, 2 * TF + 1)
                        if t.dt:
                            pool.wait_ge(cT_ps, TD + 1)
                        pool.tensor_tensor(accp[:, :], etmp[:, 0, :], etmp[:, 1, :], ALU.add).then_inc(accp_step, 1)
                    elif name == "f_e3a":
                        pool.wait_ge(etmp_ready, 2 * TF + 2)
                        pool.wait_ge(accp_step, 3 * TF + 1)
                        pool.tensor_tensor(accp[:, :], accp[:, :], etmp[:, 1, :], ALU.add).then_inc(accp_step, 1)
                        pool.wait_ge(accp_step, 3 * TF + 2)
                        pool.tensor_tensor(esum, accp[:, :], etmp[:, 0, :], ALU.add).then_inc(accp_step, 1)
                    elif name == "g_xb":
                        pool.wait_ge(x0f_loaded, 16 * (TG + 1))
                        pool.tensor_tensor(x0f, x0f, b2, ALU.add).then_inc(x0fb_ready, 1)

            walk(pool, body)

        @block.scalar
        def _(act):
            def copy(o, i, scale=1.0):
                return nc.scalar.activation(o, i, ACT.Copy, scale=scale)

            for k, w in enumerate((m_sb, wko)):
                act.wait_ge(fold_ps, k + 1)
                copy(w[:, :, :], bank[k][:, :].rearrange("p (c d) -> p c d", c=EC)).then_inc(folded, 1)

            def body(t):
                T, TR, TF, TG = t.at, t.rt, t.ft, t.gt
                if t.dt:
                    TD = GT * t.dt[0] + t.dt[1]
                for step in t.steps:
                    name = step[0]
                    if name == "st":
                        sj, hg = t.st
                        kb, h = step[1:]
                        i = kb * HJ + h
                        base = units_before(sj, hg)
                        r0 = max(0, kb - (key_tiles(sj) - GT)) * P
                        act.wait_ge(st_ready, base + i + 1)
                        if h == 0 and not (is_first(base) and kb < 2):
                            act.wait_ge(pv_done, key_tiles_before(sj, hg) + kb - 1)
                        nc.scalar.activation(pbuf[:, i % PB, r0:GQ], stbank[i % STB][:, r0:GQ], ACT.Exp)\
                            .then_inc(exp_done, 1)
                    elif name == "nm_T":
                        job = GT * t.mx[0] + t.mx[1]
                        act.wait_ge(nmT_ps, job + 1)
                        if not is_first(job):
                            act.wait_ge(nm_loaded, 16 * HJ * job)
                        copy(nmT[:, :], nmbank).then_inc(nmT_ready, 1)
                    elif name == "o_evac":
                        act.wait_ge(pv_done, key_tiles_before(*t.st) + key_tiles(t.st[0]))
                        copy(osb[:, :], obank[:, :]).then_inc(osb_ready, 1)
                    elif name == "a_xTc":
                        act.wait_ge(xT_ps, T + 1)
                        copy(xT[:, :, :], abank[:, :].rearrange("p (c t) -> p c t", c=EC)).then_inc(xT_ready, 1)
                    elif name == "a_qc":
                        act.wait_ge(qT_ps, T + 1)
                        copy(qT[:, :, :], abank[:, 0:E].rearrange("p (c t) -> p c t", c=EC), E ** -0.5)\
                            .then_inc(qT_ready, 1)
                    elif name == "a_exp":
                        act.wait_ge(nmA_ready, T + 1)
                        if t.rt is not None:
                            act.wait_ge(rxT_ps, TR + 1)
                        nc.scalar.activation(pA[:, :], abank[:, 0:2 * P], ACT.Exp, bias=nmA[:, 0:1],
                                             accum_out=sumA[:, 0:1]).then_inc(pA_ready, 1)
                    elif name == "a_pTc":
                        act.wait_ge(pT_ps, T + 1)
                        copy(pT, abank[:, 0:2 * P].rearrange("p (c t) -> p c t", c=2)).then_inc(pT_ready, 1)
                    elif name == "a_yc":
                        act.wait_ge(yT_ps, T + 1)
                        copy(yT[:, :, :], abank[:, 0:E].rearrange("p (c t) -> p c t", c=EC)).then_inc(yT_ready, 1)
                    elif name == "r_rTc":
                        act.wait_ge(rxT_ps, TR + 1)
                        copy(rxT[:, :, :], rbank(t)[:, :].rearrange("p (c t) -> p c t", c=2 * EC)).then_inc(rxT_ready, 1)
                    elif name == "d_cTc":
                        act.wait_ge(cT_ps, TD + 1)
                        copy(cT[:, :, :], dbank[:, 0:E].rearrange("p (c t) -> p c t", c=EC)).then_inc(cT_ready, 1)
                    elif name == "d_x1Tc":
                        act.wait_ge(x1T_ps, TD + 1)
                        copy(x1T[:, :, :], dbank[:, 0:E].rearrange("p (c t) -> p c t", c=EC)).then_inc(x1T_ready, 1)
                    elif name == "f_exp":
                        act.wait_ge(ngm_ready, TF + 1)
                        nc.scalar.activation(ge[:, :], lg[:, :], ACT.Exp, bias=ngm[:, 0:1], accum_out=gsum[:, 0:1])\
                            .then_inc(ge_ready, 1)
                    elif name == "f_wTc":
                        act.wait_ge(wT_ps, TF + 1)
                        copy(wT[:, :], dbank[0:NE, 0:P]).then_inc(wT_ready, 1)
                    elif name in ("f_e1c", "f_e3c"):
                        k = int(name[3])
                        act.wait_ge(e_ps, 4 * TF + k + 1)
                        if name == "f_e3c":
                            act.wait_ge(accp_step, 3 * TF + 1)
                        elif not is_first(TF):
                            act.wait_ge(out_stored, 16 * TF)
                        eb2 = expert_bank(t, k)
                        copy(etmp[:, 0, :], eb2[:, 0:E], wts[:, 2 * k:2 * k + 1])
                        copy(etmp[:, 1, :], eb2[:, E:2 * E], wts[:, 2 * k + 1:2 * k + 2]).then_inc(etmp_ready, 1)

            walk(act, body)

        @block.vector
        def _(dve):
            v = nc.vector
            v.memset(obank[:, :], 0.0).then_inc(dve_set, 1)
            v.memset(ks3[KR:KR + NPART, 0, :], 1.0).then_inc(dve_set, 1)
            dve.wait_ge(proj_loaded, 16 * PROJ_LOADS)
            v.tensor_scalar(inw[:, :, 0:E], inw[:, :, 0:E], DH ** -0.5, None, ALU.mult).then_inc(dve_set, 1)
            v.tensor_scalar(qkb[:, 0:EC], qkb[:, 0:EC], DH ** -0.5, None, ALU.mult).then_inc(dve_set, 1)
            dve.wait_ge(dve_set, 4)
            dve.wait_ge(consts, 9)

            def moments(x, st, mv, st_sem, mv_sem, n):
                v.bn_stats(st[:, :], x).then_inc(st_sem, 1)
                dve.wait_ge(st_sem, n)
                settled(dve)
                v.bn_aggr(mv[:, :], st[:, :]).then_inc(mv_sem, 1)

            def body(t):
                T, TR, TF, TG = t.at, t.rt, t.ft, t.gt
                if t.dt:
                    TD = GT * t.dt[0] + t.dt[1]
                for step in t.steps:
                    name = step[0]
                    if name == "mx":
                        sm, um = t.mx
                        c, j, h = step[1:]
                        g = keys_groups(sm)
                        i = (c * GT + j) * HJ + h
                        width = (j + 1) * P if c == g - 1 else GQ
                        dve.wait_ge(mx_ready, units_before(sm, um) + i + 1)
                        v.reduce_max(mxs[:, j * HJ + h, c:c + 1], mxbank[i % MXB][:, 0:width], AX_X)\
                            .then_inc(mx_used, 1)
                    elif name == "nm_d":
                        sm, um = t.mx
                        g = keys_groups(sm)
                        job = GT * sm + um
                        dve.wait_ge(mx_used, units_before(sm, um) + units(sm))
                        if g == 1:
                            v.tensor_scalar(nm[:, :], mxs[:, :, 0], -1.0, None, ALU.mult).then_inc(nm_step, 1)
                        else:
                            v.tensor_reduce(nm[:, :], mxs[:, :, 0:g], AX_X, ALU.max, negate=True).then_inc(nm_step, 1)
                        src = nm
                        for a in range(NPART):
                            dve.wait_ge(nm_step, NCHAINM * job + 2 * a + 1)
                            part = nmp[:, :, :, a]
                            srcv = src[:, :].rearrange("p (j h) -> p j h", j=GT)
                            v.tensor_copy(part, srcv).then_inc(nm_step, 1)
                            if a == NPART - 1:
                                break
                            if a == 0:
                                dve.wait_ge(nm_step, NCHAINM * job + 2)
                                v.tensor_tensor(nmd[:, :].rearrange("p (j h) -> p j h", j=GT), srcv, part,
                                                ALU.subtract).then_inc(nm_step, 1)
                                src = nmd
                            else:
                                dve.wait_ge(nm_step, NCHAINM * job + 4)
                                v.tensor_tensor(nmp[:, :, :, 2], srcv, part, ALU.subtract).then_inc(nm_step, 1)
                                break
                    elif name == "o_ctx":
                        sj, hg = t.st
                        job = GT * sj + hg
                        ov = dbank[:, :].rearrange("p (j h x) -> p j h x", j=GT, h=HJ)
                        dve.wait_ge(oT_ps, job + 1)
                        v.reciprocal(oden[:, :, :], ov[:, :, :, DH]).then_inc(oden_ready, 1)
                        dve.wait_ge(oden_ready, job + 1)
                        dst = ctxn[:, (sj % 2) * GT:(sj % 2 + 1) * GT, ds(hg * (HJ * DH), HJ * DH)]\
                            .rearrange("p j (h d) -> p j h d", h=HJ)
                        v.tensor_tensor(dst, ov[:, :, :, 0:DH],
                                        oden[:, :, :].unsqueeze(3).broadcast_to([P, GT, HJ, DH]), ALU.mult)\
                            .then_inc(ctx_ready, 1)
                    elif name == "a_max":
                        dve.wait_ge(sA_ps, T + 1)
                        v.tensor_reduce(nmA[:, :], abank[:, 0:2 * P], AX_X, ALU.max, negate=True)\
                            .then_inc(nmA_ready, 1)
                    elif name == "a_res":
                        dve.wait_ge(pA_ready, T + 1)
                        v.reciprocal(rsA[:, :], sumA[:, :]).then_inc(rsA_ready, 1)
                        dve.wait_ge(rsA_ready, T + 1)
                        dve.wait_ge(oA_ps, T + 1)
                        dve.wait_ge(xb_ready, T + 1)
                        v.scalar_tensor_tensor(out=rA[:, :], in0=abank[:, 0:E], scalar=rsA[:, 0:1], in1=xb[:, :],
                                               op0=ALU.mult, op1=ALU.add).then_inc(rA_ready, 1)
                        dve.wait_ge(rA_ready, T + 1)
                        moments(rA[:, :], stA, mvA, stA_ready, mvA_ready, T + 1)
                    elif name == "a_norm":
                        dve.wait_ge(rstdA_ready, T + 1)
                        dve.wait_ge(mvA_ready, T + 1)
                        if not is_first(T):
                            dve.wait_ge(x0_stored, 16 * T)
                            dve.wait_ge(rxT_ps, T)
                        v.tensor_scalar(x0[:, :], rA[:, :], mvA[:, 0:1], rstdA[:, 0:1], ALU.subtract, ALU.mult)\
                            .then_inc(x0_ready, 1)
                    elif name == "r_qkf":
                        dve.wait_ge(qk_ps, TR + 1)
                        if not is_first(TR):
                            dve.wait_ge(parts_ready, TR)
                        v.tensor_tensor(qkf[:, :, :], rbank(t)[:, :].rearrange("p (c t) -> p c t", c=2 * EC),
                                        qkb[:, :].unsqueeze(2).broadcast_to([P, 2 * EC, P]), ALU.add)\
                            .then_inc(qkf_ready, 1)
                    elif name == "r_vst":
                        dve.wait_ge(v_ps, TR + 1)
                        if not is_first(TR):
                            dve.wait_ge(v_stored, 16 * TR)
                        v.tensor_tensor(vst[:, :, 0:DH], rbank(t)[:, 0:E].rearrange("p (h d) -> p h d", h=H),
                                        b_v.rearrange("p (h d) -> p h d", h=H), ALU.add).then_inc(vst_ready, 1)
                    elif name == "d_res":
                        dve.wait_ge(oD_ps, TD + 1)
                        dve.wait_ge(x0b_ready, TD + 1)
                        v.tensor_tensor(rD[:, :], dbank[:, 0:E], x0b[:, :], ALU.add).then_inc(rD_ready, 1)
                        dve.wait_ge(rD_ready, TD + 1)
                        moments(rD[:, :], stD, mvD, stD_ready, mvD_ready, TD + 1)
                    elif name == "d_norm":
                        dve.wait_ge(mvD_ready, TD + 1)
                        v.scalar_tensor_tensor(out=rD[:, :], in0=rD[:, :], scalar=mvD[:, 0:1], in1=g1,
                                               op0=ALU.subtract, op1=ALU.mult).then_inc(xh_ready, 1)
                    elif name == "d_aff":
                        dve.wait_ge(xh_ready, TD + 1)
                        dve.wait_ge(rstdD_ready, TD + 1)
                        if not is_first(TD):
                            dve.wait_ge(acc_step, 5 * TD - 4)
                            dve.wait_ge(x1T_ps, TD)
                        v.scalar_tensor_tensor(out=x1[:, :], in0=rD[:, :], scalar=rstdD[:, 0:1], in1=b1,
                                               op0=ALU.mult, op1=ALU.add).then_inc(x1_ready, 1)
                    elif name == "f_lg":
                        if is_first(TF):
                            dve.wait_ge(moe_loaded, 16 * MOE_LOADS)
                        dve.wait_ge(g_ps, TF + 1)
                        v.tensor_tensor(lg[:, :], dbank[:, 0:NE], gb_sb[:, :], ALU.add).then_inc(lg_ready, 1)
                        dve.wait_ge(lg_ready, TF + 1)
                        v.tensor_reduce(ngm[:, :], lg[:, :], AX_X, ALU.max, negate=True).then_inc(ngm_ready, 1)
                    elif name == "f_top":
                        dve.wait_ge(ge_ready, TF + 1)
                        v.reciprocal(gr[:, :], gsum[:, :]).then_inc(top_step, 1)
                        dve.wait_ge(top_step, NTOP * TF + 1)
                        v.tensor_scalar(gates[:, :], ge[:, :], gr[:, 0:1], None, ALU.mult).then_inc(top_step, 1)
                        dve.wait_ge(top_step, NTOP * TF + 2)
                        settled(dve)
                        v.max(top8[:, :], gates[:, :]).then_inc(top_step, 1)
                        dve.wait_ge(top_step, NTOP * TF + 3)
                        settled(dve)
                        v.max_index(ix8[:, :], top8[:, :], gates[:, :]).then_inc(top_step, 1)
                        dve.wait_ge(top_step, NTOP * TF + 4)
                        v.tensor_copy(ixf[:, :], ix8[:, :]).then_inc(top_step, 1)
                        dve.wait_ge(top_step, NTOP * TF + 5)
                        for k, w in enumerate((w1st, w2nd)):
                            v.scalar_tensor_tensor(out=w[:, :], in0=iota8[:, :], scalar=ixf[:, k:k + 1],
                                                   in1=gates[:, :], op0=ALU.is_equal, op1=ALU.mult)\
                                .then_inc(top_step, 1)
                        dve.wait_ge(top_step, NTOP * TF + 7)
                        v.tensor_tensor(wts[:, :], w1st[:, :], w2nd[:, :], ALU.add).then_inc(wts_ready, 1)
                    elif name == "f_acc0":
                        dve.wait_ge(eb_ps, TF + 1)
                        dve.wait_ge(x1_ready, TF + 1)
                        if not is_first(TF):
                            dve.wait_ge(z_ready, TF)
                        v.tensor_tensor(acc[:, :], dbank[:, 0:E], x1[:, :], ALU.add).then_inc(acc_step, 1)
                    elif name in ("f_e0c", "f_e2c"):
                        k = int(name[3])
                        dve.wait_ge(e_ps, 4 * TF + k + 1)
                        for e in range(2):
                            dve.wait_ge(acc_step, 5 * TF + k + e + 1)
                            v.scalar_tensor_tensor(out=acc[:, :], in0=expert_bank(t, k)[:, e * E:(e + 1) * E],
                                                   scalar=wts[:, 2 * k + e:2 * k + e + 1], in1=acc[:, :],
                                                   op0=ALU.mult, op1=ALU.add).then_inc(acc_step, 1)
                    elif name == "g_y":
                        dve.wait_ge(accp_step, 3 * TG + 3)
                        dve.wait_ge(acc_step, 5 * TG + 5)
                        v.tensor_tensor(acc[:, :], acc[:, :], esum, ALU.add).then_inc(y_ready, 1)
                        dve.wait_ge(y_ready, TG + 1)
                        moments(acc[:, :], stF, mvF, stF_ready, mvF_ready, 2 * TG + 1)
                    elif name == "g_norm2":
                        dve.wait_ge(mvF_ready, 2 * TG + 1)
                        v.scalar_tensor_tensor(out=acc[:, :], in0=acc[:, :], scalar=mvF[:, 0:1], in1=g2,
                                               op0=ALU.subtract, op1=ALU.mult).then_inc(xh2_ready, 1)
                    elif name == "g_aff2":
                        dve.wait_ge(xh2_ready, TG + 1)
                        dve.wait_ge(rstdF_ready, 2 * TG + 1)
                        dve.wait_ge(x0fb_ready, TG + 1)
                        v.scalar_tensor_tensor(out=esum, in0=acc[:, :], scalar=rstdF[:, 0:1], in1=x0f,
                                               op0=ALU.mult, op1=ALU.add).then_inc(z_ready, 1)
                    elif name == "g_z":
                        dve.wait_ge(z_ready, TG + 1)
                        moments(esum, stF, mvF, stF_ready, mvF_ready, 2 * TG + 2)
                    elif name == "g_norm3":
                        dve.wait_ge(rstdF_ready, 2 * TG + 2)
                        dve.wait_ge(mvF_ready, 2 * TG + 2)
                        v.tensor_scalar(obuf, esum, mvF[:, 0:1], rstdF[:, 0:1], ALU.subtract, ALU.mult)\
                            .then_inc(ob_ready, 1)

            walk(dve, body)

        @block.tensor
        def _(pe):
            mm, tr = nc.tensor.matmul, nc.tensor.transpose
            pe.wait_ge(fold_loaded, 16 * FOLD_LOADS)
            wqkt = pbuf[:, 0:2, :].rearrange("p a b -> p (a b)").rearrange("p (c d) -> p c d", c=2 * EC)
            woutn = pbuf[:, 2, :].rearrange("p (c d) -> p c d", c=EC)
            for k, (lc, rhs) in enumerate(((0, wqkt[:, EC:2 * EC, :]), (EC, woutn))):
                for d in range(EC):
                    for e in range(EC):
                        last = mm(bank[k][:, d * E:(d + 1) * E], wqkt[:, lc + e, d * P:(d + 1) * P], rhs[:, e, :],
                                  start=e == 0, stop=e == EC - 1)
                last.then_inc(fold_ps, 1)
            pe.wait_ge(folded, 2)
            pe.wait_ge(consts, 9)
            pe.wait_ge(dve_set, 4)

            def wait_context_bank(t):
                pe.wait_ge(ctx_ready, GT * t.st[0] + t.st[1] if t.st else GT * NG)

            def body(t):
                T, TR, TF, TG = t.at, t.rt, t.ft, t.gt
                if t.dt:
                    TD = GT * t.dt[0] + t.dt[1]
                for step in t.steps:
                    name = step[0]
                    if name == "mx":
                        sm, um = t.mx
                        c, j, h = step[1:]
                        g = keys_groups(sm)
                        i = (c * GT + j) * HJ + h
                        base = units_before(sm, um)
                        diag = c == g - 1
                        width = (j + 1) * P if diag else GQ
                        if i == 0 and is_first(base):
                            pe.wait_ge(vst_ready, GT + 1)
                        if i == 0 and is_first(um):
                            pe.wait_ge(stack_loaded, 16 * 2 * SLOTS * GT * (sm + 1))
                        if i >= MXB:
                            pe.wait_ge(mx_used, base + i - MXB + 1)
                        elif not is_first(base):
                            pe.wait_ge(mx_used, base)
                        qcol = (um * HJ + h) * (QRING * GQ) + (sm % QRING) * GQ + j * P
                        kcol = (um * HJ + h) * (KRING * GQ) + (((sm // GB) * GB + c) % KRING) * GQ
                        bk = mxbank[i % MXB]
                        last = mm(bk[:, 0:width], qs[0:KR, ds(qcol, P)], ks[0:KR, ds(kcol, width)],
                                  start=True, stop=not diag)
                        if diag:
                            last = mm(bk[:, j * P:(j + 1) * P], idb[:, :], maskb[:, :], start=False, stop=True)
                        last.then_inc(mx_ready, 1)
                    elif name == "nm_T":
                        job = GT * t.mx[0] + t.mx[1]
                        pe.wait_ge(nm_step, NCHAINM * (job + 1))
                        if t.at is not None:
                            pe.wait_ge(rA_ready, T + 1)
                        elif t.rt is not None:
                            pe.wait_ge(vst_ready, TR + 1)
                        elif not is_first(job):
                            pe.wait_ge(nmT_ready, job)
                        for j in range(GT):
                            last = tr(nmbank[:, j * P:(j + 1) * P],
                                      nmp[:, j, :, :].rearrange("p h a -> p (h a)"), idb[:, :])
                        last.then_inc(nmT_ps, 1)
                    elif name == "st":
                        sj, hg = t.st
                        kb, h = step[1:]
                        i = kb * HJ + h
                        base = units_before(sj, hg)
                        first_diag = key_tiles(sj) - GT
                        r0 = max(0, kb - first_diag) * P
                        if i == 0 and is_first(base):
                            pe.wait_ge(ones_loaded, 16)
                        if i == 0:
                            pe.wait_ge(nm_loaded, 16 * HJ * (GT * sj + hg + 1))
                        if i >= STB:
                            pe.wait_ge(exp_done, base + i - STB + 1)
                        elif not is_first(base):
                            pe.wait_ge(exp_done, base)
                        kcol = (hg * HJ + h) * (KRING * GQ) + (((sj // GB) * GB + kb // GT) % KRING) * GQ + kb % GT * P
                        qcol = (hg * HJ + h) * (QRING * GQ) + (sj % QRING) * GQ + r0
                        bk = stbank[i % STB]
                        last = mm(bk[:, r0:GQ], ks[0:KR + NPART, ds(kcol, P)], qs[0:KR + NPART, ds(qcol, GQ - r0)],
                                  start=True, stop=kb < first_diag)
                        if kb >= first_diag:
                            last = mm(bk[:, r0:r0 + P], maskb[:, :], idb[:, :], start=False, stop=True)
                        last.then_inc(st_ready, 1)
                    elif name == "pv":
                        sj, hg = t.st
                        kb = step[1]
                        last_kb = key_tiles(sj) - 1
                        jj = kb - (last_kb + 1 - GT)
                        r0 = max(0, jj) * P
                        job = GT * sj + hg
                        pe.wait_ge(exp_done, units_before(sj, hg) + HJ * (kb + 1))
                        if kb % GT == 0:
                            pe.wait_ge(vcur_loaded[kb // GT], 16 * (loads_before(sj, hg, kb // GT) + 1))
                        if kb == 0 and not is_first(job):
                            pe.wait_ge(osb_ready, job)
                        for h in range(HJ):
                            last = mm(obank[32 * h:32 * h + DV, r0:GQ], vcur[:, kb, h, :],
                                      pbuf[:, (kb * HJ + h) % PB, r0:GQ], start=kb == 0, stop=kb == last_kb,
                                      tile_position=(0, 32 * h))
                        last.then_inc(pv_done, 1)
                    elif name == "o_T":
                        job = GT * t.st[0] + t.st[1]
                        pe.wait_ge(osb_ready, job + 1)
                        if t.dt:
                            pe.wait_ge(x1T_ready, TD + 1)
                        elif t.ft is not None:
                            pe.wait_ge(etmp_ready, 2 * (TF + 1))
                        elif not is_first(job):
                            pe.wait_ge(ctx_ready, job)
                        for j in range(GT):
                            last = tr(dbank[:, j * P:(j + 1) * P], osb[:, j * P:(j + 1) * P], idf[:, :])
                        last.then_inc(oT_ps, 1)
                    elif name == "a_xT":
                        pe.wait_ge(xw_loaded, 16 * (T + 1))
                        if t.mx and not is_first(t.mx[1] + GT * t.mx[0]):
                            pe.wait_ge(nmT_ready, GT * t.mx[0] + t.mx[1])
                        elif not is_first(T):
                            pe.wait_ge(rA_ready, T)
                        for c in range(EC):
                            for w in range(2):
                                last = tr(abank[:, (2 * c + w) * P:(2 * c + w + 1) * P], xw[:, w, c * P:(c + 1) * P],
                                          idf[:, :])
                        last.then_inc(xT_ps, 1)
                    elif name == "a_q":
                        pe.wait_ge(xT_ready, T + 1)
                        for co in range(EC):
                            for ci in range(EC):
                                last = mm(abank[:, co * P:(co + 1) * P], m_sb[:, ci, co * P:(co + 1) * P],
                                          xT[:, ci, P:2 * P], start=ci == 0, stop=ci == EC - 1)
                        last.then_inc(qT_ps, 1)
                    elif name == "a_s":
                        pe.wait_ge(qT_ready, T + 1)
                        if t.mx and t.rt is not None:
                            pe.wait_ge(rxT_ready, TR + 1)
                        for c in range(EC):
                            mm(abank[:, 0:2 * P], qT[:, c, :], xT[:, c, :], start=c == 0, stop=False)
                        mm(abank[:, P:2 * P], idb[:, :], maskb[:, :], start=False, stop=True).then_inc(sA_ps, 1)
                    elif name == "a_pT":
                        pe.wait_ge(pA_ready, T + 1)
                        if t.mx and t.rt is not None:
                            pe.wait_ge(qkf_ready, TR + 1)
                        for w in range(2):
                            last = tr(abank[:, w * P:(w + 1) * P], pA[:, w * P:(w + 1) * P], idf[:, :])
                        last.then_inc(pT_ps, 1)
                    elif name == "a_y":
                        pe.wait_ge(pT_ready, T + 1)
                        if t.mx and t.rt is not None:
                            pe.wait_ge(vst_ready, TR + 1)
                        for c in range(EC):
                            for w in range(2):
                                last = mm(abank[:, c * P:(c + 1) * P], xw[:, w, c * P:(c + 1) * P], pT[:, w, :],
                                          start=w == 0, stop=w == 1)
                        last.then_inc(yT_ps, 1)
                    elif name == "a_o":
                        pe.wait_ge(yT_ready, T + 1)
                        for c in range(EC):
                            last = mm(abank[:, 0:E], yT[:, c, :], wko[:, c, :], start=c == 0, stop=c == EC - 1)
                        last.then_inc(oA_ps, 1)
                    elif name == "r_rT":
                        pe.wait_ge(rp_ready, TR + 1)
                        if not t.mx:
                            if not is_first(TR):
                                pe.wait_ge(vst_ready, TR)
                        elif t.at is not None:
                            pe.wait_ge(qT_ready, T + 1)
                        else:
                            pe.wait_ge(nmT_ready, GT * t.mx[0] + t.mx[1])
                        for c in range(2 * EC):
                            src = (rp if c < EC else x0)[:, (c % EC) * P:(c % EC + 1) * P]
                            last = tr(rbank(t)[:, c * P:(c + 1) * P], src, idf[:, :])
                        last.then_inc(rxT_ps, 1)
                    elif name == "r_qk":
                        pe.wait_ge(rxT_ready, TR + 1)
                        if t.mx and t.at is not None:
                            pe.wait_ge(pA_ready, T + 1)
                        for co in range(2 * EC):
                            for ci in range(EC):
                                last = mm(rbank(t)[:, co * P:(co + 1) * P], inw[:, ci, co * P:(co + 1) * P],
                                          rxT[:, ci, :], start=ci == 0, stop=ci == EC - 1)
                        last.then_inc(qk_ps, 1)
                    elif name == "r_v":
                        if t.mx and t.at is not None:
                            pe.wait_ge(pT_ready, T + 1)
                        else:
                            pe.wait_ge(qkf_ready, TR + 1)
                        for ci in range(EC):
                            last = mm(rbank(t)[:, 0:E], rxT[:, EC + ci, :], inw[:, ci, 2 * E:3 * E],
                                      start=ci == 0, stop=ci == EC - 1)
                        last.then_inc(v_ps, 1)
                    elif name == "d_cT":
                        pe.wait_ge(cj_ready, TD + 1)
                        if t.ft is not None:
                            pe.wait_ge(lg_ready, TF + 1)
                        else:
                            wait_context_bank(t)
                        for c in range(EC):
                            last = tr(dbank[:, c * P:(c + 1) * P], cj[:, c * P:(c + 1) * P], idf[:, :])
                        last.then_inc(cT_ps, 1)
                    elif name == "d_o":
                        pe.wait_ge(cT_ready, TD + 1)
                        if is_first(TD):
                            pe.wait_ge(moe_loaded, 16 * MOE_LOADS)
                        for c in range(EC):
                            last = mm(dbank[:, 0:E], cT[:, c, :], wo[:, c, :], start=c == 0, stop=c == EC - 1)
                        last.then_inc(oD_ps, 1)
                    elif name == "d_x1T":
                        pe.wait_ge(x1_ready, TD + 1)
                        if t.ft is not None:
                            pe.wait_ge(etmp_ready, 2 * (TF + 1))
                            if not t.mx:
                                pe.wait_ge(acc_step, 5 * TF + 1)
                        for c in range(EC):
                            last = tr(dbank[:, c * P:(c + 1) * P], x1[:, c * P:(c + 1) * P], idf[:, :])
                        last.then_inc(x1T_ps, 1)
                    elif name == "f_g":
                        pe.wait_ge(x1T_ready, TF + 1)
                        wait_context_bank(t)
                        for c in range(EC):
                            last = mm(dbank[:, 0:NE], x1T[:, c, :], gw[:, c, :], start=c == 0, stop=c == EC - 1)
                        last.then_inc(g_ps, 1)
                    elif name == "f_wT":
                        pe.wait_ge(wts_ready, TF + 1)
                        if t.dt:
                            pe.wait_ge(rD_ready, TD + 1)
                        tr(dbank[0:NE, 0:P], wts[:, :], idf[:, :]).then_inc(wT_ps, 1)
                    elif name == "f_b":
                        pe.wait_ge(wT_ready, TF + 1)
                        mm(dbank[:, 0:E], wT[:, :], eb[:, :], start=True, stop=True).then_inc(eb_ps, 1)
                    elif name in ("f_e0", "f_e1", "f_e2", "f_e3"):
                        k = int(name[3])
                        if t.mx:
                            if k in (0, 1, 3):
                                pe.wait_ge(acc_step, 5 * TF + (1, 3, None, 5)[k])
                            else:
                                pe.wait_ge(etmp_ready, 2 * TF + 1)
                        else:
                            pe.wait_ge((acc_step, etmp_ready)[k % 2], (5 * TF, 2 * TF, 5 * TF + 3, 2 * TF + 1)[k])
                        for c in range(EC):
                            last = mm(expert_bank(t, k)[:, :], x1T[:, c, :], ew[:, c, k * 2 * E:(k + 1) * 2 * E],
                                      start=c == 0, stop=c == EC - 1)
                        last.then_inc(e_ps, 1)

            walk(pe, body)


def kernel(L0_attn_x, L0_attn_w_qkv, L0_attn_w_out, L0_attn_b_out, L0_ffn_in_proj_w, L0_ffn_in_proj_b,
           L0_ffn_out_proj_w, L0_ffn_out_proj_b, L0_ffn_gate_w, L0_ffn_gate_b, L0_ffn_expert_w, L0_ffn_expert_b,
           L0_ffn_ln1_w, L0_ffn_ln1_b, L0_ffn_ln2_w, L0_ffn_ln2_b):
    import concourse.bacc as bacc
    from concourse.bass_utils import run_bass_kernel_spmd as run

    windows = np.zeros((NT + 1, 2, P, E), np.float32)
    tiles = np.asarray(L0_attn_x).reshape(B, TB, P, E)
    windows[:NT, 1] = tiles.reshape(NT, P, E)
    windows[:NT, 0].reshape(B, TB, P, E)[:, 1:] = tiles[:, :-1]
    inv_freq = (1.0 / np.float32(10000.0) ** (np.arange(0, DH, 2, dtype=np.float32) / np.float32(DH)))
    freqs = np.arange(N, dtype=np.float32)[:, None] * inv_freq.astype(np.float32)[None, :]
    cs = np.zeros((N, 2, DH // 2, 2), np.float32)
    cs[:, 0, :, 0] = cs[:, 0, :, 1] = np.cos(freqs)
    cs[:, 1, :, 1] = np.sin(freqs)
    cs[:, 1, :, 0] = -np.sin(freqs)
    rows = np.empty((P, 7, E), np.float32)
    for i, vec in enumerate((L0_attn_b_out, np.asarray(L0_ffn_in_proj_b)[2 * E:], L0_ffn_out_proj_b, L0_ffn_ln1_w,
                             L0_ffn_ln1_b, L0_ffn_ln2_w, L0_ffn_ln2_b)):
        rows[:, i, :] = np.asarray(vec)
    arrays = {
        "windows": windows.reshape((NT + 1) * 2 * P, E),
        "cs": np.concatenate([cs.reshape(N, 2 * DH)] * B + [np.zeros((P, 2 * DH), np.float32)]),
        "w_qk_t": np.asarray(L0_attn_w_qkv)[:, :2 * E].T,
        "w_out": np.asarray(L0_attn_w_out),
        "in_t": np.asarray(L0_ffn_in_proj_w).T,
        "in_b": np.asarray(L0_ffn_in_proj_b)[:2 * E].reshape(2 * EC, P).T,
        "wo_t": np.asarray(L0_ffn_out_proj_w).T,
        "gate_t": np.asarray(L0_ffn_gate_w).T,
        "exp_t": np.asarray(L0_ffn_expert_w).transpose(2, 0, 1).reshape(E, NE * E),
        "exp_b": np.asarray(L0_ffn_expert_b),
        "rows": rows,
        "gate_b": np.broadcast_to(np.asarray(L0_ffn_gate_b)[None, :], (P, NE)),
    }
    arrays = {n: np.ascontiguousarray(a) for n, a in arrays.items()}
    nc = bacc.Bacc("TRN2", target_bir_lowering=False, num_devices=1)
    args = [nc.dram_tensor(n, a.shape, mybir.dt.from_np(a.dtype), kind="ExternalInput").ap()
            for n, a in arrays.items()]
    args.append(nc.dram_tensor("out", (NT * P, E), F32, kind="ExternalOutput").ap())
    build(nc, *args)
    r = run(nc, [arrays], core_ids=[0])
    return r.results[0]["out"].reshape(B, N, E)
```
